# Optimizing a Trainium2 kernel written in Bass

```python
import numpy as np
import jax
import jax.numpy as jnp

def _softmax(x, axis=-1):
    return jax.nn.softmax(x, axis=axis)

def _gelu(x):
    return jax.nn.gelu(x, approximate=True)

def _silu(x):
    return jax.nn.silu(x)

def _sigmoid(x):
    return jax.nn.sigmoid(x)

def _layernorm(x, axis=-1, eps=1e-05):
    m = jnp.mean(x, axis=axis, keepdims=True)
    v = jnp.var(x, axis=axis, keepdims=True)
    return (x - m) / jnp.sqrt(v + eps)

def _scatter_add(tgt, idx, src, axis=0):
    return tgt.at[idx].add(src)

def _segment_sum(src, seg, n):
    return jax.ops.segment_sum(src, seg, n)
kernel_name = 'mk_prb_d1_jaxref_r8_80b134'

def setup_inputs(seed: int=0):
    np.random.seed(seed)
    _w = jnp.asarray

    def _L0_attn_setup():
        import jax, jax.numpy as jnp
        import numpy as np
        EMBED_DIM = 128
        K_DIM = 128
        MAX_SEQ_LEN = 256
        key = jax.random.key(seed)
        ks = jax.random.split(key, 9)
        s = 0.02
        x = jax.random.normal(ks[0], (4, 256, EMBED_DIM), dtype=jnp.float32)
        wq = jax.random.normal(ks[1], (EMBED_DIM, K_DIM), dtype=jnp.float32) * s
        bq = jnp.zeros((K_DIM,), dtype=jnp.float32)
        wk = jax.random.normal(ks[2], (EMBED_DIM, K_DIM), dtype=jnp.float32) * s
        bk = jnp.zeros((K_DIM,), dtype=jnp.float32)
        wv = jax.random.normal(ks[3], (EMBED_DIM, K_DIM), dtype=jnp.float32) * s
        bv = jnp.zeros((K_DIM,), dtype=jnp.float32)
        wo = jax.random.normal(ks[4], (K_DIM, EMBED_DIM), dtype=jnp.float32) * s
        bo = jnp.zeros((EMBED_DIM,), dtype=jnp.float32)
        return {'x': x, 'wq': wq, 'bq': bq, 'wk': wk, 'bk': bk, 'wv': wv, 'bv': bv, 'wo': wo, 'bo': bo}
    _L0_attn_in = _L0_attn_setup()

    def _L0_ffn_setup():
        import jax, jax.numpy as jnp
        import numpy as np
        E = 32
        K = 4
        H = 128
        F = 128
        LIMIT = 7.0
        ALPHA = 1.702
        EPS = 1e-05

        def _rmsnorm(x, scale):
            t = x * jax.lax.rsqrt(jnp.mean(x * x, axis=-1, keepdims=True) + EPS)
            return t * scale

        def _swiglu(h):
            glu = jnp.minimum(h[..., ::2], LIMIT)
            lin = jnp.clip(h[..., 1::2], -LIMIT, LIMIT)
            return glu * jax.nn.sigmoid(ALPHA * glu) * (lin + 1.0)
        key = jax.random.key(seed)
        ks = jax.random.split(key, 8)
        B, S = (1, 128)
        x = jax.random.normal(ks[0], (B, S, H), dtype=jnp.float32)
        norm_scale = jnp.ones((H,), dtype=jnp.float32)
        gate_w = jax.random.normal(ks[1], (E, H), dtype=jnp.float32) * 0.02
        gate_b = jnp.zeros((E,), dtype=jnp.float32)
        w1 = jax.random.normal(ks[2], (E, 2 * F, H), dtype=jnp.float32) * 0.02
        b1 = jnp.zeros((E, 2 * F), dtype=jnp.float32)
        w2 = jax.random.normal(ks[3], (E, H, F), dtype=jnp.float32) * 0.02
        b2 = jnp.zeros((E, H), dtype=jnp.float32)
        return {'x': x, 'norm_scale': norm_scale, 'gate_w': gate_w, 'gate_b': gate_b, 'w1': w1, 'b1': b1, 'w2': w2, 'b2': b2}
    _L0_ffn_in = _L0_ffn_setup()
    _d = {'L0_attn_x': _L0_attn_in['x'], 'L0_attn_wq': _L0_attn_in['wq'], 'L0_attn_bq': _L0_attn_in['bq'], 'L0_attn_wk': _L0_attn_in['wk'], 'L0_attn_bk': _L0_attn_in['bk'], 'L0_attn_wv': _L0_attn_in['wv'], 'L0_attn_bv': _L0_attn_in['bv'], 'L0_attn_wo': _L0_attn_in['wo'], 'L0_attn_bo': _L0_attn_in['bo'], 'L0_ffn_norm_scale': _L0_ffn_in['norm_scale'], 'L0_ffn_gate_w': _L0_ffn_in['gate_w'], 'L0_ffn_gate_b': _L0_ffn_in['gate_b'], 'L0_ffn_w1': _L0_ffn_in['w1'], 'L0_ffn_b1': _L0_ffn_in['b1'], 'L0_ffn_w2': _L0_ffn_in['w2'], 'L0_ffn_b2': _L0_ffn_in['b2']}
    _x0 = _d['L0_attn_x']
    _d['L0_attn_x'] = jax.random.normal(jax.random.fold_in(jax.random.key(seed), 1), (4, 1024, 128), dtype=_x0.dtype)
    del _x0
    return _d

def reference(L0_attn_x, L0_attn_wq, L0_attn_bq, L0_attn_wk, L0_attn_bk, L0_attn_wv, L0_attn_bv, L0_attn_wo, L0_attn_bo, L0_ffn_norm_scale, L0_ffn_gate_w, L0_ffn_gate_b, L0_ffn_w1, L0_ffn_b1, L0_ffn_w2, L0_ffn_b2):

    def _L0_attn_ref(x, wq, bq, wk, bk, wv, bv, wo, bo):
        import jax, jax.numpy as jnp
        import numpy as np
        EMBED_DIM = 128
        K_DIM = 128
        MAX_SEQ_LEN = 256
        B, S, D = x.shape
        scale = jnp.asarray(K_DIM ** 0.5, x.dtype)
        Q = x @ wq + bq
        K = x @ wk + bk
        V = x @ wv + bv
        scores = jnp.einsum('bqk,bsk->bqs', Q, K) / scale
        row = jnp.arange(S)[:, None]
        col = jnp.arange(S)[None, :]
        mask = col <= row + 1
        scores = jnp.where(mask, jnp.asarray(-1000000000.0, scores.dtype), scores)
        attn = jax.nn.softmax(scores, axis=-1)
        out = jnp.einsum('bqs,bsk->bqk', attn, V)
        return out @ wo + bo

    def _L0_ffn_ref(x, norm_scale, gate_w, gate_b, w1, b1, w2, b2):
        import jax, jax.numpy as jnp
        import numpy as np
        E = 32
        K = 4
        H = 128
        F = 128
        LIMIT = 7.0
        ALPHA = 1.702
        EPS = 1e-05

        def _rmsnorm(x, scale):
            t = x * jax.lax.rsqrt(jnp.mean(x * x, axis=-1, keepdims=True) + EPS)
            return t * scale

        def _swiglu(h):
            glu = jnp.minimum(h[..., ::2], LIMIT)
            lin = jnp.clip(h[..., 1::2], -LIMIT, LIMIT)
            return glu * jax.nn.sigmoid(ALPHA * glu) * (lin + 1.0)
        B, S, _ = x.shape
        t = _rmsnorm(x, norm_scale)
        g = t @ gate_w.T + gate_b
        tf = t.reshape(-1, H)
        gf = g.reshape(-1, E)
        T = tf.shape[0]
        vals, idx = jax.lax.top_k(gf, K)
        w = jax.nn.softmax(vals, axis=-1)
        combine = jnp.zeros((T, E), dtype=tf.dtype).at[jnp.arange(T)[:, None], idx].add(w)
        h1 = jnp.einsum('th,efh->tef', tf, w1) + b1
        h = _swiglu(h1)
        hw = h * combine[:, :, None]
        out = jnp.einsum('tef,ehf->th', hw, w2) + combine @ b2
        return x + out.reshape(B, S, H)
    x = L0_attn_x
    xn = _layernorm(x, axis=-1)
    x = x + _L0_attn_ref(xn, L0_attn_wq, L0_attn_bq, L0_attn_wk, L0_attn_bk, L0_attn_wv, L0_attn_bv, L0_attn_wo, L0_attn_bo) + _L0_ffn_ref(xn, L0_ffn_norm_scale, L0_ffn_gate_w, L0_ffn_gate_b, L0_ffn_w1, L0_ffn_b1, L0_ffn_w2, L0_ffn_b2)
    return x

_drawn_inputs = setup_inputs


def setup_inputs(seed=0):
    import zlib

    import numpy as np

    out = dict(_drawn_inputs(seed))
    spreads = {'L0_attn_bq': (0.0, 0.8),
     'L0_attn_bk': (0.0, 2.0),
     'L0_attn_bv': (0.0, 0.753),
     'L0_attn_bo': (0.0, 0.368),
     'L0_ffn_norm_scale': (1.0, 0.6),
     'L0_ffn_gate_b': (0.0, 0.423),
     'L0_ffn_b1': (0.0, 0.8),
     'L0_ffn_b2': (0.0, 0.318)}
    factors = {'L0_attn_wq': 8.0,
     'L0_attn_wk': 8.0,
     'L0_attn_wv': 8.0,
     'L0_attn_wo': 5.777,
     'L0_ffn_w1': 7.878,
     'L0_ffn_w2': 7.195}
    for name, (base, spread) in spreads.items():
        noise = np.random.default_rng([zlib.crc32(name.encode()), seed]).standard_normal(out[name].shape)
        drawn = base * np.exp(spread * noise) if base else spread * noise
        out[name] = jnp.asarray(drawn.astype(out[name].dtype))
    for name, factor in factors.items():
        out[name] = (out[name] * factor).astype(out[name].dtype)
    return out
```

```python
from contextlib import ExitStack

import concourse.bass as bass
from concourse import mybir

F32 = mybir.dt.float32
BF16 = mybir.dt.bfloat16
I32 = mybir.dt.int32
U32 = mybir.dt.uint32
ALU = mybir.AluOpType
ACT = mybir.ActivationFunctionType
AX = mybir.AxisListType

P = 128
D = 128
BATCHES = 4
SEQ = 1024
TOKENS = BATCHES * SEQ
TILES = TOKENS // P
BT = SEQ // P
E = 32
K = 4
CAP = TOKENS + P
SLOT_TILES = 160
ROW = D + 2
DEST, WEIGHT = D, D + 1
NOWHERE = 1 << 20
DUMMY = E * CAP
WCOLS = 3 * D + 2
U = 8
SCALE = float(D) ** -0.5
MASKED = -1.0e9
LIMIT, ALPHA = 7.0, 1.702
EPS = 1e-5
SPREAD = K * BT

ROUTE = 17
PT_AT = [0, 2, 4, 6, 8, 9, 10, 11, 12]


def layer(nc, x, wqkv, bq, bk, bv, wo, bo, norm_scale, gate_wT, gate_b, experts, b2, out):
    slots = nc.dram_tensor("slots", [DUMMY + P, ROW], F32).ap()
    parts = nc.dram_tensor("parts", [TOKENS * K, D], F32).ap()
    plan_dram = nc.dram_tensor("plan", [2 * P, 2], I32).ap()

    ctx = ExitStack()
    with ctx:
        def sb(name, shape, dt=F32):
            return ctx.enter_context(nc.sbuf_tensor(name, shape, dt))

        def sem(name):
            return ctx.enter_context(nc.semaphore(name))

        xs = sb("xs", [P, TILES, D])
        wqkv_s = sb("wqkv_s", [P, 3, D])
        wo_s = sb("wo_s", [P, D])
        bias_s = sb("bias_s", [P, 3])
        bq_scaled = sb("bq_scaled", [P, 1])
        bv_b = sb("bv_b", [P, D])
        scale_b = sb("scale_b", [P, D])
        gate_b_b = sb("gate_b_b", [P, E])
        gate_raw = sb("gate_raw", [P, E])
        gate_s = sb("gate_s", [P, E])
        b2_s = sb("b2_s", [E + 1, D])
        ident = sb("ident", [P, P])
        earlier = sb("earlier", [P, P], BF16)
        ones_bf = sb("ones_bf", [P, P], BF16)
        ones2 = sb("ones2", [P, 2])
        iota_e = sb("iota_e", [P, E])
        iota_i = sb("iota_i", [P, E], I32)
        cap_mask = sb("cap_mask", [P, 2 * P])
        extra = sb("extra", [P, 1])
        id_i = sb("id_i", [P, SPREAD], I32)
        ids = sb("ids", [P, SPREAD])
        tile_no_i = sb("tile_no_i", [P, 2], I32)
        tile_no = sb("tile_no", [P, 2])
        pad_rows = sb("pad_rows", [P, ROW])

        bnst = sb("bnst", [P, BT, 6])
        mv = sb("mv", [P, TILES, 2])
        stat = sb("stat", [P, 3, TILES])
        nv = sb("nv", [P, 2, TILES])
        nu = sb("nu", [P, TILES])
        nbits = sb("nbits", [P, TILES], I32)
        st_b = sb("st_b", [P, 2, 3, BT])

        xn = sb("xn", [P, 2, BT, D])
        tt = sb("tt", [P, BT, D])
        xnT = sb("xnT", [P, SEQ])
        qT = sb("qT", [P, SEQ])
        kT = sb("kT", [P, SEQ])
        v = sb("v", [P, BT, D])
        lg = sb("lg", [P, BT, E])
        mx = sb("mx", [P, BT, 8])
        mi = sb("mi", [P, BT, 8], U32)
        dlt = sb("dlt", [P, BT, K])
        ex = sb("ex", [P, BT, K])
        esum = sb("esum", [P, BT])
        erec = sb("erec", [P, BT])
        wk = sb("wk", [P, BT, K])
        idxf = sb("idxf", [P, BT, K])
        onehot = sb("onehot", [P, SPREAD, E])
        cw = sb("cw", [P, SPREAD, E])
        member = sb("member", [P, BT, E], BF16)
        seen = sb("seen", [P, E], BF16)
        seen_add = sb("seen_add", [P, E])
        comb = sb("comb", [P, BT, P])
        combT = sb("combT", [E + 1, SEQ])
        rank = sb("rank", [P, SPREAD])
        pos = sb("pos", [P, 2, SPREAD], U32)
        pay = sb("pay", [P, 2, SPREAD, ROW])

        prob = sb("prob", [P, 2, SEQ])
        probT = sb("probT", [P, 2, SEQ])
        neg_m = sb("neg_m", [P, BT])
        rsum = sb("rsum", [P, BT])
        rden = sb("rden", [P, BT])
        oT = sb("oT", [P, 2, P])

        cnt = sb("cnt", [P, E])
        nt_i = sb("nt_i", [P, E], I32)
        nt_s = sb("nt_s", [P, E], I32)
        nt = sb("nt", [P, E])
        ct = sb("ct", [P, E])
        one_row = sb("one_row", [P, E])
        ge = sb("ge", [P, 2, E])
        gt = sb("gt", [P, 2, E])
        eidx = sb("eidx", [P, 2])
        excl = sb("excl", [P, 2])
        loc = sb("loc", [P, 2])
        row_f = sb("row_f", [P, 2])
        plan = sb("plan_s", [P, 2, 2], I32)
        plan_row = sb("plan_row", [1, 4 * P], I32)
        pad_at = sb("pad_at", [P, E], I32)

        wx = sb("wx", [P, U, WCOLS])
        xg = sb("xg", [P, U, ROW])
        xgT = sb("xgT", [P, 2, P])
        hg = sb("hg", [P, 2, P])
        hl = sb("hl", [P, 2, P])
        hl1 = sb("hl1", [P, 2, P])
        sl = sb("sl", [P, 2, P])
        hw = sb("hw", [P, 2, P])
        ye = sb("ye", [P, U, D])
        CH = 4
        yl = sb("yl", [P, 2, CH, K, D])
        ya = sb("ya", [P, CH, 2, D])
        yb = sb("yb", [P, CH, D])

        big = ctx.enter_context(nc.psum_tensor("big", [P, 2, 1024], F32))
        mid = ctx.enter_context(nc.psum_tensor("mid", [P, 2, 512], F32))
        o_ps_t = ctx.enter_context(nc.psum_tensor("o_ps_t", [P, 512], F32))
        rt_ps_t = ctx.enter_context(nc.psum_tensor("rt_ps_t", [P, 512], F32))
        lg_ps_v = rt_ps_t[:, 0:BT * E].rearrange("p (j e) -> p j e", e=E)
        rank_ps_v = rt_ps_t[:, 256:256 + BT * E].rearrange("p (j e) -> p j e", e=E)

        x_loaded = [sem(f"x_loaded{b}") for b in range(BATCHES)]
        const_loaded = sem("const_loaded")
        pool_const = sem("pool_const")
        dve_const = sem("dve_const")
        stats = sem("stats")
        xn_done, t_done, base_done, st_done = sem("xn_done"), sem("t_done"), sem("base_done"), sem("st_done")
        lg_done, top_done, route = sem("lg_done"), sem("top_done"), sem("route")
        v_done, masked, smax, ot_done = sem("v_done"), sem("masked"), sem("smax"), sem("ot_done")
        den_done, acc_done, b2_added = sem("den_done"), sem("acc_done"), sem("b2_added")
        xnT_ps, lg_ps, proj_ps, rank_ps = sem("xnT_ps"), sem("lg_ps"), sem("proj_ps"), sem("rank_ps")
        s_ps, pt_ps, o_ps, pr_ps = sem("s_ps"), sem("pt_ps"), sem("o_ps"), sem("pr_ps")
        ct_ps, b2_ps, cnt_ps = sem("ct_ps"), sem("b2_ps"), sem("cnt_ps")
        xnT_done, qk_done, ex_done, pay_done = sem("xnT_done"), sem("qk_done"), sem("ex_done"), sem("pay_done")
        p_done, pt_done, ct_done = sem("p_done"), sem("pt_done"), sem("ct_done")
        pool_go, dve_go = sem("pool_go"), sem("dve_go")
        scattered = [sem(f"scattered{h}") for h in range(2)]
        planned, plan_out, plan_back = sem("planned"), sem("plan_out"), sem("plan_back")
        padded = sem("padded")
        tile_in = [sem(f"tile_in{u}") for u in range(U)]
        xg_ps, xg_done, h_ps, g_done = sem("xg_ps"), sem("xg_done"), sem("h_ps"), sem("g_done")
        l_done, sl_done, hw_done = sem("l_done"), sem("sl_done"), sem("hw_done")
        y_ps, y_done = sem("y_ps"), sem("y_done")
        returned = [sem(f"returned{u}") for u in range(U)]
        sum_in = [sem(f"sum_in{b}") for b in range(2)]
        summed, stored = sem("summed"), sem("stored")

        NCONST = 11

        block = ctx.enter_context(nc.Block())

        def bcast(ap, shape):
            return ap.broadcast_to(shape)

        @block.sync
        def _(sp):
            x_v = x.rearrange("(i p) d -> p i d", p=P)
            sp.dma_start(xs[:, 0:BT, :], x_v[:, 0:BT, :]).then_inc(x_loaded[0], 16)
            sp.dma_start(wqkv_s[:], wqkv).then_inc(const_loaded, 16)
            sp.dma_start(bias_s[:, 0:1], bq).then_inc(const_loaded, 16)
            sp.dma_start(bias_s[:, 1:2], bk).then_inc(const_loaded, 16)
            sp.dma_start(bias_s[:, 2:3], norm_scale).then_inc(const_loaded, 16)
            sp.dma_start(gate_raw[:], gate_wT).then_inc(const_loaded, 16)
            sp.dma_start(gate_b_b[:], gate_b.partition_broadcast(P)).then_inc(const_loaded, 16)
            sp.dma_start(scale_b[:], norm_scale.rearrange("d a -> (d a)").partition_broadcast(P)).then_inc(const_loaded, 16)
            sp.dma_start(bv_b[:], bv.partition_broadcast(P)).then_inc(const_loaded, 16)
            sp.dma_start(wo_s[:], wo).then_inc(const_loaded, 16)
            sp.dma_start(b2_s[0:E, :], b2).then_inc(const_loaded, 16)
            sp.dma_start(b2_s[E:E + 1, :], bo).then_inc(const_loaded, 16)
            for b in range(1, BATCHES):
                sp.dma_start(xs[:, b * BT:(b + 1) * BT, :], x_v[:, b * BT:(b + 1) * BT, :]).then_inc(x_loaded[b], 16)

            sp.wait_ge(planned, 13)
            sp.dma_start(plan_dram.rearrange("(q p) c -> p q c", p=P), plan[:]).then_inc(plan_out, 16)
            sp.wait_ge(pool_const, PAD_READY)
            sp.dma_start(slots[DUMMY:DUMMY + P, :], pad_rows[:]).then_inc(padded, 16)
            with sp.Fori(0, E) as e:
                at = sp.value_load(pad_at[0:1, bass.ds(e, 1)], min_val=0, max_val=DUMMY - P)
                sp.dma_start(slots[bass.ds(at, P), :], pad_rows[:]).then_inc(padded, 16)
            sp.wait_ge(plan_out, 16)
            sp.dma_start(plan_row[:], plan_dram.rearrange("(a n) c -> a (n c)", a=1)).then_inc(plan_back, 16)
            sp.wait_ge(plan_back, 16)
            sp.wait_ge(padded, 16 * (E + 1))
            for h in range(2):
                sp.wait_ge(scattered[h], 16 * SPREAD * 2)

            with sp.Fori(0, SLOT_TILES // U) as it:
                for u in range(U):
                    sp.wait_ge(returned[u], 16 * it)
                    n = it * U + u
                    e = sp.value_load(plan_row[0:1, bass.ds(n * 2, 1)], min_val=0, max_val=E - 1)
                    at = sp.value_load(plan_row[0:1, bass.ds(n * 2 + 1, 1)], min_val=0, max_val=DUMMY)
                    sp.dma_start(xg[:, u, :], slots[bass.ds(at, P), :]).then_inc(tile_in[u], 16)
                    sp.dma_start(wx[:, u, :], experts[bass.ds(e, 1), :, :].rearrange("a p n -> (a p) n"))\
                      .then_inc(tile_in[u], 16)
            for u in range(U):
                sp.wait_ge(returned[u], 16 * (SLOT_TILES // U))
            parts_v = parts.rearrange("(i p k) d -> p i (k d)", p=P, k=K)
            out_v = out.rearrange("(i p) d -> p i d", p=P)
            n_chunks = TILES // CH
            for q in range(n_chunks + 1):
                if q < n_chunks:
                    if q >= 2:
                        sp.wait_ge(summed, 3 * (q - 1))
                    sp.dma_start(yl[:, q % 2].rearrange("p i k d -> p i (k d)"),
                                 parts_v[:, q * CH:(q + 1) * CH, :]).then_inc(sum_in[q % 2], 16)
                if q >= 1:
                    sp.wait_ge(summed, 3 * q)
                    sp.dma_start(out_v[:, (q - 1) * CH:q * CH, :], xs[:, (q - 1) * CH:q * CH, :]).then_inc(stored, 16)
            sp.wait_ge(stored, 16 * n_chunks)

        @block.gpsimd
        def _(pool):
            made = [0]

            def const(ins, then=True):
                made[0] += 1
                ins.then_inc(pool_const, 1)
                if then:
                    pool.wait_ge(pool_const, made[0])

            const(pool.memset(ident[:], 0.0))
            const(pool.affine_select(out=ident[:], in_=ident[:], compare_op=ALU.not_equal, fill=1.0, base=0,
                                     pattern=[[-1, P]], channel_multiplier=1), False)
            const(pool.memset(ones_bf[:], 1.0))
            const(pool.affine_select(out=earlier[:], in_=ones_bf[:], compare_op=ALU.is_gt, fill=0.0, base=0,
                                     pattern=[[1, P]], channel_multiplier=-1), False)
            const(pool.iota(iota_i[:], [[1, E]], base=0, channel_multiplier=0), False)
            const(pool.iota(id_i[:], [[K * P, BT], [1, K]], base=0, channel_multiplier=K), False)
            const(pool.iota(tile_no_i[:], [[P, 2]], base=0, channel_multiplier=1), False)
            const(pool.memset(cap_mask[:], 3.0e38))
            const(pool.affine_select(out=cap_mask[:], in_=cap_mask[:], compare_op=ALU.is_ge, fill=MASKED, base=-2,
                                     pattern=[[1, 2 * P]], channel_multiplier=-1), False)
            const(pool.memset(extra[:], float(SEQ - P)))
            const(pool.affine_select(out=extra[:], in_=extra[:], compare_op=ALU.is_ge, fill=0.0, base=-(P - 2),
                                     pattern=[[0, 1]], channel_multiplier=1), False)
            const(pool.memset(pad_rows[:], 0.0), False)
            const(pool.memset(one_row[:], 1.0))
            const(pool.iota(pad_rows[:, DEST:DEST + 1].bitcast(I32), [[0, 1]], base=NOWHERE, channel_multiplier=0))
            assert made[0] == PAD_READY

            slot_limit = pool.to_reg(DUMMY - 1)
            part_limit = pool.to_reg(TOKENS * K - 1)
            with pool.Fori(0, BATCHES // 2) as it:
                for h in range(2):
                    c = it * 2 + h
                    pool.wait_ge(pay_done, BT * (c + 1))
                    pool.sem_inc(pool_go, 1)
                    pool.wait_ge(route, ROUTE * c + POS_DONE)
                    pool.sem_inc(pool_go, 1)
                    for n in range(SPREAD):
                        pool.indirect_dma_start(slots, bass.IndirectOffsetOnAxis(pos[:, h, n:n + 1], 0),
                                                pay[:, h, n, :], None, bounds_check=slot_limit, oob_is_err=False)\
                            .then_inc(scattered[h], 16)
            with pool.Fori(0, SLOT_TILES // U) as it:
                for u in range(U):
                    pool.wait_ge(y_done, it * U + u + 1)
                    pool.sem_inc(pool_go, 1)
                    pool.indirect_dma_start(parts, bass.IndirectOffsetOnAxis(xg[:, u, DEST:DEST + 1].bitcast(U32), 0),
                                            ye[:, u, :], None, bounds_check=part_limit, oob_is_err=False)\
                        .then_inc(returned[u], 16)

        @block.tensor
        def _(pe):
            pe.wait_ge(const_loaded, 16 * NCONST)
            pe.wait_ge(pool_const, PAD_READY)
            pe.wait_ge(dve_const, DVE_CONST)

            def scores(c, i):
                w = SEQ - P * i
                if i < 2:
                    pe.wait_ge(qk_done, 4 * c + 4)
                else:
                    pe.wait_ge(p_done, BT * c + i - 1)
                for a in range(0, w, 512):
                    n = min(512, w - a)
                    last = pe.matmul(big[:, i % 2, a:a + n], qT[:, P * i:P * i + P],
                                     kT[:, P * i + a:P * i + a + n], start=True, stop=True)
                last.then_inc(s_ps, 1)

            def transpose_probs(c, i):
                pe.wait_ge(p_done, BT * c + i + 1)
                if i == 0:
                    pe.wait_ge(v_done, 2 * c + 2)
                else:
                    pe.wait_ge(pt_done, 12 * c + PT_AT[i])
                nb = BT - i
                for m in range((nb + 3) // 4):
                    for j in range(4 * m, min(nb, 4 * m + 4)):
                        last = pe.transpose(mid[:, m, P * (j % 4):P * (j % 4) + P],
                                            prob[:, i % 2, P * j:P * j + P], ident[:])
                    last.then_inc(pt_ps, 1)

            def values(c, i):
                pe.wait_ge(pt_done, 12 * c + PT_AT[i + 1])
                pe.wait_ge(ot_done, BT * c + i)
                o = o_ps_t[:, 0:P]
                nb = BT - i
                for j in range(nb):
                    last = pe.matmul(o, v[:, i + j, :], probT[:, i % 2, P * j:P * j + P],
                                     start=(j == 0), stop=(j == nb - 1 and i < BT - 1))
                if i == BT - 1:
                    for j in range(BT - 1):
                        last = pe.matmul(o[:, P - 2:P], v[:, j, :], ones2[:], start=False, stop=(j == BT - 2))
                last.then_inc(o_ps, 1)

            def project(c, i):
                pe.wait_ge(ot_done, BT * c + i + 1)
                pe.wait_ge(acc_done, BT * c + i)
                pe.matmul(rt_ps_t[:, 0:D], oT[:, i % 2, :], wo_s[:],
                          start=True, stop=True).then_inc(pr_ps, 1)

            with pe.Fori(0, BATCHES // 2) as it:
                for h in range(2):
                    c = it * 2 + h
                    pe.wait_ge(pt_done, 12 * c)
                    for g in range(2):
                        pe.wait_ge(xn_done, BT * c + 4 * (g + 1))
                        for j in range(4):
                            last = pe.transpose(mid[:, g, P * j:P * j + P], xn[:, h, 4 * g + j, :], ident[:])
                        last.then_inc(xnT_ps, 1)
                    pe.wait_ge(xnT_done, 2 * c + 2)
                    pe.wait_ge(acc_done, BT * c)
                    for j in range(BT):
                        last = pe.matmul(lg_ps_v[:, j, :], xnT[:, P * j:P * j + P], gate_s[:], start=True, stop=True)
                    last.then_inc(lg_ps, 1)
                    pe.wait_ge(ct_done, 2 * c)
                    pe.wait_ge(b2_added, c)
                    for g in range(2):
                        for w in range(2):
                            pe.matmul(big[:, g, 512 * w:512 * w + 512], wqkv_s[:, w, :],
                                      xnT[:, 512 * g:512 * g + 512], start=True, stop=True).then_inc(proj_ps, 1)
                        for j in range(4):
                            last = pe.matmul(mid[:, g, P * j:P * j + P], xnT[:, P * (4 * g + j):P * (4 * g + j + 1)],
                                             wqkv_s[:, 2, :], start=True, stop=True)
                        last.then_inc(proj_ps, 1)
                    pe.wait_ge(route, ROUTE * c + 4)
                    pe.matmul(rank_ps_v, ones_bf[:], bcast(seen[:].unsqueeze(1), [P, BT, E]), start=True, stop=False)
                    for j in range(BT - 1):
                        pe.matmul(rank_ps_v[:, j + 1:BT, :], ones_bf[:],
                                  bcast(member[:, j, :].unsqueeze(1), [P, BT - 1 - j, E]), start=False, stop=False)
                    pe.matmul(rank_ps_v, earlier[:], member[:], start=False, stop=True).then_inc(rank_ps, 1)

                    scores(c, 0)
                    scores(c, 1)
                    for i in range(BT + 2):
                        if i < BT:
                            transpose_probs(c, i)
                        if i + 2 < BT:
                            scores(c, i + 2)
                        if 0 <= i - 1 < BT:
                            values(c, i - 1)
                        if 0 <= i - 2 < BT:
                            project(c, i - 2)
                        if i == BT:
                            pe.wait_ge(p_done, BT * c + BT)
                            pe.wait_ge(route, ROUTE * c + ROUTE)
                            for j in range(BT):
                                last = pe.transpose(big[:, 0, P * j:P * j + P], comb[:, j, :], ident[:])
                                if j % 4 == 3:
                                    last.then_inc(ct_ps, 1)
                    pe.wait_ge(ct_done, 2 * c + 2)
                    for j in range(BT):
                        last = pe.matmul(big[:, 1, P * j:P * j + P], combT[:, P * j:P * j + P], b2_s[:],
                                         start=True, stop=True)
                    last.then_inc(b2_ps, 1)
            pe.wait_ge(route, ROUTE * BATCHES)
            pe.wait_ge(acc_done, BT * BATCHES)
            pe.matmul(rt_ps_t[:, 0:E], ones_bf[:], seen[:], start=True, stop=True).then_inc(cnt_ps, 1)

            def tile_T(it, u):
                n = it * U + u
                pe.wait_ge(tile_in[u], 32 * it + 32)
                pe.wait_ge(xg_done, n - 1 if u >= 1 else it * U)
                pe.transpose(big[:, u % 2, 0:P], xg[:, u, 0:D], ident[:]).then_inc(xg_ps, 1)

            def tile_H(it, u):
                n = it * U + u
                pe.wait_ge(xg_done, n + 1)
                pe.wait_ge(l_done, 2 * n - 2 if u >= 1 else it * (2 * U))
                pe.matmul(big[:, u % 2, 512:512 + P], wx[:, u, 0:D], xgT[:, u % 2, :], start=True, stop=True)
                pe.matmul(big[:, u % 2, 512 + P:512 + 2 * P], wx[:, u, D:2 * D], xgT[:, u % 2, :],
                          start=True, stop=True).then_inc(h_ps, 1)

            def tile_Y(it, u):
                n = it * U + u
                pe.wait_ge(hw_done, n + 1)
                pe.wait_ge(y_done, n - 1 if u >= 1 else it * U)
                pe.matmul(mid[:, u % 2, 0:D], hw[:, u % 2, :], wx[:, u, 2 * D:3 * D],
                          start=True, stop=True).then_inc(y_ps, 1)

            pe.wait_ge(ct_done, 2 * BATCHES)
            pe.wait_ge(b2_added, BATCHES)
            pe.wait_ge(pt_done, 12 * BATCHES)
            turns = SLOT_TILES // U
            for u in range(3):
                tile_T(0, u)
                if u >= 1:
                    tile_H(0, u - 1)

            def turn(it, last):
                for u in range(U):
                    if not (last and u + 3 >= U):
                        tile_T(it + (u + 3) // U, (u + 3) % U)
                    if not (last and u + 2 >= U):
                        tile_H(it + (u + 2) // U, (u + 2) % U)
                    tile_Y(it, u)

            with pe.Fori(0, turns - 1) as it:
                turn(it, False)
            turn(turns - 1, True)

        @block.scalar
        def _(act):
            act.wait_ge(const_loaded, 16 * NCONST)
            act.wait_ge(dve_const, DVE_CONST)

            def payload(c, h, j):
                act.wait_ge(t_done, BT * c + j + 1)
                act.copy(pay[:, h, K * j:K * j + K, 0:D], bcast(tt[:, j, :].unsqueeze(1), [P, K, D]))\
                   .then_inc(pay_done, 1)

            def qk(c, g, w):
                act.wait_ge(proj_ps, 6 * c + 3 * g + w + 1)
                act.activation((qT, kT)[w][:, 512 * g:512 * g + 512], big[:, g, 512 * w:512 * w + 512], ACT.Identity,
                               bias=(bq_scaled[:, 0:1], bias_s[:, 1:2])[w], scale=(SCALE, 1.0)[w]).then_inc(qk_done, 1)

            def exps(c, i):
                act.wait_ge(smax, BT * c + i + 1)
                act.wait_ge(pt_ps, 12 * c + (PT_AT[i - 1] if i >= 2 else 0))
                w = SEQ - P * i
                act.activation(prob[:, i % 2, 0:w], big[:, i % 2, 0:w], ACT.Exp, bias=neg_m[:, i:i + 1],
                               accum_out=rsum[:, i:i + 1]).then_inc(p_done, 1)

            def probs_T(c, i):
                act.wait_ge(o_ps, BT * c + max(i - 1, 0))
                nb = BT - i
                for m in range((nb + 3) // 4):
                    n = P * min(4, nb - 4 * m)
                    act.wait_ge(pt_ps, 12 * c + PT_AT[i] + m + 1)
                    act.copy(probT[:, i % 2, 512 * m:512 * m + n], mid[:, m, 0:n]).then_inc(pt_done, 1)

            with act.Fori(0, BATCHES // 2) as it:
                for h in range(2):
                    c = it * 2 + h
                    for g in range(2):
                        act.wait_ge(xnT_ps, 2 * c + g + 1)
                        act.copy(xnT[:, 512 * g:512 * g + 512], mid[:, g, :]).then_inc(xnT_done, 1)
                    act.wait_ge(scattered[h], 16 * SPREAD * it)
                    for j in range(4):
                        payload(c, h, j)
                    qk(c, 0, 0)
                    qk(c, 0, 1)
                    payload(c, h, 4)
                    payload(c, h, 5)
                    act.wait_ge(route, ROUTE * c + 1)
                    act.activation(ex[:], dlt[:], ACT.Exp).then_inc(ex_done, 1)
                    qk(c, 1, 0)
                    qk(c, 1, 1)
                    payload(c, h, 6)
                    payload(c, h, 7)
                    exps(c, 0)
                    for i in range(BT):
                        if i + 1 < BT:
                            exps(c, i + 1)
                        probs_T(c, i)
                    for g in range(2):
                        act.wait_ge(ct_ps, 2 * c + g + 1)
                        act.copy(combT[:, 512 * g:512 * g + 512], big[0:E + 1, 0, 512 * g:512 * g + 512])\
                           .then_inc(ct_done, 1)

            def tile_X(it, u):
                n = it * U + u
                act.wait_ge(xg_ps, n + 1)
                act.wait_ge(h_ps, n - 1 if u >= 1 else it * U)
                act.copy(xgT[:, u % 2, :], big[:, u % 2, 0:P]).then_inc(xg_done, 1)

            def tile_S(it, u):
                n = it * U + u
                act.wait_ge(g_done, n + 1)
                act.wait_ge(hw_done, n - 1 if u >= 1 else it * U)
                act.activation(sl[:, u % 2, :], hg[:, u % 2, :], ACT.Silu, scale=ALPHA).then_inc(sl_done, 1)

            def tile_E(it, u):
                n = it * U + u
                act.wait_ge(y_ps, n + 1)
                act.activation(ye[:, u, :], mid[:, u % 2, 0:D], ACT.Copy, scale=xg[:, u, WEIGHT:WEIGHT + 1])\
                   .then_inc(y_done, 1)

            turns = SLOT_TILES // U
            for u in range(3):
                tile_X(0, u)
                if u >= 1:
                    tile_S(0, u - 1)

            def turn(it, last):
                for u in range(U):
                    if not (last and u + 3 >= U):
                        tile_X(it + (u + 3) // U, (u + 3) % U)
                    if not (last and u + 2 >= U):
                        tile_S(it + (u + 2) // U, (u + 2) % U)
                    tile_E(it, u)

            with act.Fori(0, turns - 1) as it:
                turn(it, False)
            turn(turns - 1, True)

        @block.vector
        def _(dve):
            n_const = [0]

            def const(ins):
                n_const[0] += 1
                ins.then_inc(dve_const, 1)

            dve.wait_ge(pool_const, PAD_READY)
            const(dve.tensor_copy(iota_e[:], iota_i[:]))
            const(dve.tensor_copy(ids[:], id_i[:]))
            const(dve.tensor_copy(tile_no[:], tile_no_i[:]))
            const(dve.memset(ones2[:], 1.0))
            const(dve.memset(seen[:], 0.0))
            const(dve.memset(comb[:], 0.0))
            dve.wait_ge(dve_const, n_const[0])
            const(dve.memset(comb[:, :, E:E + 1], 1.0))
            dve.wait_ge(const_loaded, 16 * NCONST)
            const(dve.tensor_scalar(bq_scaled[:], bias_s[:, 0:1], SCALE, None, ALU.mult))
            const(dve.tensor_scalar(gate_s[:], gate_raw[:], bias_s[:, 2:3], None, ALU.mult))
            assert n_const[0] == DVE_CONST

            n_stat = [0]

            def stat_step(ins, wait=True):
                n_stat[0] += 1
                ins.then_inc(stats, 1)
                if wait:
                    dve.wait_ge(stats, n_stat[0])

            for b in range(BATCHES):
                dve.wait_ge(x_loaded[b], 16)
                for j in range(BT):
                    stat_step(dve.bn_stats(bnst[:, j, :], xs[:, b * BT + j, :]), j == BT - 1)
                for j in range(BT):
                    stat_step(dve.bn_aggr(mv[:, b * BT + j, :], bnst[:, j, :]), j == BT - 1)

            def inv_sqrt(dst, a, tmp, tmp2):
                stat_step(dve.tensor_scalar(nbits[:], a.bitcast(I32), -0.5, float(0x5F3759DF), ALU.mult, ALU.add))
                guess = nbits[:].bitcast(F32)
                for step in range(4):
                    stat_step(dve.tensor_tensor(tmp, guess, guess, ALU.mult))
                    stat_step(dve.tensor_tensor(tmp2, tmp, a, ALU.mult))
                    stat_step(dve.tensor_scalar(tmp, tmp2, -0.5, 1.5, ALU.mult, ALU.add))
                    stat_step(dve.tensor_tensor(dst, guess, tmp, ALU.mult))
                    guess = dst

            stat_step(dve.tensor_copy(stat[:, 0, :], mv[:, :, 0]), False)
            stat_step(dve.tensor_scalar(nu[:], mv[:, :, 1], EPS, None, ALU.add))
            inv_sqrt(stat[:, 1, :], nu[:], nv[:, 0, :], nv[:, 1, :])
            stat_step(dve.tensor_tensor(nv[:, 0, :], stat[:, 1, :], stat[:, 1, :], ALU.mult))
            stat_step(dve.tensor_tensor(nv[:, 1, :], nv[:, 0, :], mv[:, :, 1], ALU.mult))
            stat_step(dve.tensor_scalar(nu[:], nv[:, 1, :], EPS, None, ALU.add))
            inv_sqrt(stat[:, 2, :], nu[:], nv[:, 0, :], nv[:, 1, :])

            def mask_max(c, i):
                w = SEQ - P * i
                wm = min(w, 2 * P)
                dve.wait_ge(s_ps, BT * c + i + 1)
                dve.tensor_tensor(big[:, i % 2, 0:wm], big[:, i % 2, 0:wm], cap_mask[:, 0:wm], ALU.min)\
                   .then_inc(masked, 1)
                dve.wait_ge(masked, BT * c + i + 1)
                dve.tensor_reduce(neg_m[:, i:i + 1], big[:, i % 2, 0:w], AX.X, ALU.max, negate=True).then_inc(smax, 1)

            with dve.Fori(0, BATCHES // 2) as it:
                for h in range(2):
                    c = it * 2 + h
                    xs_c = xs[:, bass.ds(c * BT, BT), :]

                    def routed(k):
                        dve.wait_ge(route, ROUTE * c + k)

                    dve.tensor_copy(st_b[:, h], stat[:, :, bass.ds(c * BT, BT)]).then_inc(st_done, 1)
                    dve.wait_ge(st_done, c + 1)
                    for j in range(BT):
                        dve.tensor_scalar(xn[:, h, j, :], xs[:, bass.ds(c * BT + j, 1), :].rearrange("p a d -> p (a d)"),
                                          st_b[:, h, 0, j:j + 1], st_b[:, h, 1, j:j + 1], ALU.subtract, ALU.mult)\
                           .then_inc(xn_done, 1)
                    dve.wait_ge(pay_done, BT * c)
                    dve.wait_ge(xn_done, BT * c + BT)
                    for j in range(BT):
                        dve.scalar_tensor_tensor(tt[:, j, :], xn[:, h, j, :], st_b[:, h, 2, j:j + 1], scale_b[:],
                                                 ALU.mult, ALU.mult).then_inc(t_done, 1)
                    dve.tensor_tensor(xs_c, xs_c, xn[:, h], ALU.add).then_inc(base_done, 1)

                    dve.wait_ge(lg_ps, c + 1)
                    for j in range(BT):
                        dve.scalar_tensor_tensor(lg[:, j, :], lg_ps_v[:, j, :], st_b[:, h, 2, j:j + 1], gate_b_b[:],
                                                 ALU.mult, ALU.add).then_inc(lg_done, 1)
                    dve.wait_ge(lg_done, BT * c + BT)
                    dve.sem_inc(dve_go, 1)
                    for j in range(BT):
                        dve.max(mx[:, j, :], lg[:, j, :]).then_inc(top_done, 1)
                    dve.wait_ge(top_done, 2 * BT * c + BT)
                    dve.sem_inc(dve_go, 1)
                    for j in range(BT):
                        dve.max_index(mi[:, j, :], mx[:, j, :], lg[:, j, :]).then_inc(top_done, 1)
                    dve.tensor_tensor(dlt[:], mx[:, :, 0:K], bcast(mx[:, :, 0:1], [P, BT, K]), ALU.subtract)\
                       .then_inc(route, 1)
                    dve.wait_ge(top_done, 2 * BT * c + 2 * BT)
                    dve.tensor_copy(idxf[:], mi[:, :, 0:K]).then_inc(route, 1)
                    routed(2)
                    dve.tensor_tensor(onehot[:], bcast(iota_e[:].unsqueeze(1), [P, SPREAD, E]),
                                      bcast(idxf[:].rearrange("p j k -> p (j k)").unsqueeze(2), [P, SPREAD, E]),
                                      ALU.is_equal).then_inc(route, 1)
                    routed(3)
                    with nc.allow_low_precision(reason="zeros and ones are exact"):
                        dve.tensor_reduce(member[:], onehot[:].rearrange("p (j k) e -> p j e k", k=K), AX.X, ALU.add)\
                           .then_inc(route, 1)
                    for g in range(2):
                        dve.wait_ge(proj_ps, 6 * c + 3 * g + 3)
                        dve.tensor_tensor(v[:, 4 * g:4 * g + 4, :], mid[:, g, :].rearrange("p (j d) -> p j d", d=D),
                                          bcast(bv_b[:].unsqueeze(1), [P, 4, D]), ALU.add).then_inc(v_done, 1)
                        if g == 0:
                            dve.wait_ge(ex_done, c + 1)
                            dve.tensor_reduce(esum[:], ex[:], AX.X, ALU.add).then_inc(route, 1)
                            routed(5)
                            dve.reciprocal(erec[:], esum[:]).then_inc(route, 1)
                            routed(6)
                            dve.tensor_tensor(wk[:], ex[:], bcast(erec[:].unsqueeze(2), [P, BT, K]), ALU.mult)\
                               .then_inc(route, 1)
                            dve.wait_ge(scattered[h], 16 * SPREAD * it)
                            routed(7)
                            dve.tensor_scalar(pay[:, h, :, WEIGHT:WEIGHT + 1],
                                              wk[:].rearrange("p j k -> p (j k)").unsqueeze(2), 1.0 / ALPHA, None, ALU.mult)\
                               .then_inc(route, 1)
                            dve.tensor_copy(pay[:, h, :, DEST:DEST + 1].bitcast(I32), ids[:].unsqueeze(2))\
                               .then_inc(route, 1)
                            routed(9)
                            dve.tensor_scalar(ids[:], ids[:], float(K * SEQ), None, ALU.add).then_inc(route, 1)
                    dve.wait_ge(rank_ps, c + 1)
                    dve.tensor_tensor(cw[:].rearrange("p (j k) e -> p j k e", k=K),
                                      onehot[:].rearrange("p (j k) e -> p j k e", k=K),
                                      bcast(rank_ps_v.unsqueeze(2), [P, BT, K, E]), ALU.mult).then_inc(route, 1)
                    routed(11)
                    dve.tensor_reduce(rank[:], cw[:], AX.X, ALU.add).then_inc(route, 1)
                    routed(12)
                    dve.scalar_tensor_tensor(pos[:, h, :], idxf[:].rearrange("p j k -> p (j k)"), float(CAP), rank[:],
                                             ALU.mult, ALU.add).then_inc(route, 1)
                    mask_max(c, 0)
                    mask_max(c, 1)
                    dve.tensor_tensor(cw[:], onehot[:], bcast(wk[:].rearrange("p j k -> p (j k)").unsqueeze(2),
                                                              [P, SPREAD, E]), ALU.mult).then_inc(route, 1)
                    routed(14)
                    dve.tensor_reduce(comb[:, :, 0:E], cw[:].rearrange("p (j k) e -> p j e k", k=K), AX.X, ALU.add)\
                       .then_inc(route, 1)
                    dve.tensor_reduce(seen_add[:], member[:].rearrange("p j e -> p e j"), AX.X, ALU.add)\
                       .then_inc(route, 1)
                    routed(16)
                    dve.tensor_tensor(seen[:], seen[:], seen_add[:], ALU.add).then_inc(route, 1)

                    for i in range(BT + 2):
                        if i + 2 < BT:
                            mask_max(c, i + 2)
                        if 0 <= i - 1 < BT:
                            k = i - 1
                            dve.wait_ge(o_ps, BT * c + k + 1)
                            dve.tensor_copy(oT[:, k % 2, :], o_ps_t[:, 0:P])\
                               .then_inc(ot_done, 1)
                        if 0 <= i - 2 < BT:
                            k = i - 2
                            if k == BT - 1:
                                dve.tensor_tensor(rsum[:, k:k + 1], rsum[:, k:k + 1], extra[:], ALU.add)\
                                   .then_inc(den_done, 1)
                                dve.wait_ge(den_done, (BT + 1) * c + BT)
                            dve.reciprocal(rden[:, k:k + 1], rsum[:, k:k + 1]).then_inc(den_done, 1)
                            dve.wait_ge(den_done, (BT + 1) * c + k + (2 if k == BT - 1 else 1))
                            dve.wait_ge(pr_ps, BT * c + k + 1)
                            row = xs[:, bass.ds(c * BT + k, 1), :].rearrange("p a d -> p (a d)")
                            dve.scalar_tensor_tensor(row, rt_ps_t[:, 0:D],
                                                     rden[:, k:k + 1], row, ALU.mult, ALU.add).then_inc(acc_done, 1)
                    dve.wait_ge(b2_ps, c + 1)
                    dve.wait_ge(acc_done, BT * c + BT)
                    dve.tensor_tensor(xs_c, xs_c, big[:, 1, :].rearrange("p (j d) -> p j d", d=D), ALU.add)\
                       .then_inc(b2_added, 1)

            n_plan = [0]

            def plan_step(ins):
                n_plan[0] += 1
                ins.then_inc(planned, 1)
                dve.wait_ge(planned, n_plan[0])

            dve.wait_ge(cnt_ps, 1)
            plan_step(dve.tensor_copy(cnt[:], rt_ps_t[:, 0:E]))
            plan_step(dve.tensor_scalar(nt_i[:], cnt[:], float(P - 1), None, ALU.add))
            plan_step(dve.tensor_scalar(nt_s[:], nt_i[:], 7, None, ALU.logical_shift_right))
            plan_step(dve.tensor_copy(nt[:], nt_s[:]))
            plan_step(dve.tensor_tensor_scan(ct[:], one_row[:], nt[:], 0.0, ALU.mult, ALU.add))
            plan_step(dve.tensor_tensor(ge[:], bcast(ct[:].unsqueeze(1), [P, 2, E]),
                                        bcast(tile_no[:].unsqueeze(2), [P, 2, E]), ALU.is_le))
            plan_step(dve.tensor_reduce(eidx[:], ge[:], AX.X, ALU.add))
            plan_step(dve.tensor_tensor(gt[:], ge[:], bcast(nt[:].unsqueeze(1), [P, 2, E]), ALU.mult))
            plan_step(dve.tensor_reduce(excl[:], gt[:], AX.X, ALU.add))
            plan_step(dve.tensor_tensor(loc[:], tile_no[:], excl[:], ALU.subtract))
            plan_step(dve.tensor_scalar(row_f[:], eidx[:], float(CAP), None, ALU.mult))
            plan_step(dve.scalar_tensor_tensor(loc[:], loc[:], float(P), row_f[:], ALU.mult, ALU.add))
            n_plan[0] += 0
            dve.tensor_scalar(plan[:, :, 0], eidx[:], float(E - 1), None, ALU.min).then_inc(st_done, 1)
            dve.tensor_scalar(plan[:, :, 1], loc[:], float(DUMMY), None, ALU.min).then_inc(st_done, 1)
            plan_step(dve.scalar_tensor_tensor(pad_at[:], iota_e[:], float(CAP), cnt[:], ALU.mult, ALU.add))

            def tile_HW(it, u):
                n = it * U + u
                dve.wait_ge(sl_done, n + 1)
                dve.wait_ge(l_done, 2 * n + 2)
                dve.wait_ge(y_ps, n - 1 if u >= 1 else it * U)
                dve.tensor_tensor(hw[:, u % 2, :], hl1[:, u % 2, :], sl[:, u % 2, :], ALU.mult).then_inc(hw_done, 1)

            def tile_G(it, u):
                n = it * U + u
                dve.wait_ge(h_ps, n + 1)
                dve.wait_ge(sl_done, n - 1 if u >= 1 else it * U)
                dve.tensor_scalar(hg[:, u % 2, :], big[:, u % 2, 512:512 + P], wx[:, u, 3 * D:3 * D + 1], LIMIT,
                                  ALU.add, ALU.min).then_inc(g_done, 1)
                dve.tensor_scalar(hl[:, u % 2, :], big[:, u % 2, 512 + P:512 + 2 * P], wx[:, u, 3 * D + 1:3 * D + 2],
                                  LIMIT, ALU.add, ALU.min).then_inc(l_done, 1)
                dve.wait_ge(l_done, 2 * n + 1)
                dve.tensor_scalar(hl1[:, u % 2, :], hl[:, u % 2, :], -LIMIT, 1.0, ALU.max, ALU.add).then_inc(l_done, 1)

            turns = SLOT_TILES // U
            for u in range(2):
                tile_G(0, u)

            def turn(it, last):
                for u in range(U):
                    tile_HW(it, u)
                    if not (last and u + 2 >= U):
                        tile_G(it + (u + 2) // U, (u + 2) % U)

            with dve.Fori(0, turns - 1) as it:
                turn(it, False)
            turn(turns - 1, True)

            for q in range(TILES // CH):
                dve.wait_ge(sum_in[q % 2], 16 * (q // 2 + 1))
                y = yl[:, q % 2]
                dve.tensor_tensor(ya[:], y[:, :, 0:2, :], y[:, :, 2:4, :], ALU.add).then_inc(summed, 1)
                dve.wait_ge(summed, 3 * q + 1)
                dve.tensor_tensor(yb[:], ya[:, :, 0, :], ya[:, :, 1, :], ALU.add).then_inc(summed, 1)
                dve.wait_ge(summed, 3 * q + 2)
                rows = xs[:, q * CH:(q + 1) * CH, :]
                dve.tensor_tensor(rows, rows, yb[:], ALU.add).then_inc(summed, 1)
                dve.wait_ge(summed, 3 * q + 3)


PAD_READY = 14
DVE_CONST = 9
POS_DONE = 13


def kernel(**inputs):
    import numpy as np
    import concourse.bacc as bacc
    from concourse.bass_utils import run_bass_kernel_spmd

    a = {n.replace("L0_attn_", "").replace("L0_ffn_", "f_"): np.asarray(v) for n, v in inputs.items()}
    w1 = a["f_w1"].reshape(E, D, 2, D)
    b1 = a["f_b1"].reshape(E, D, 2)
    experts = np.concatenate([w1[:, :, 0].transpose(0, 2, 1), w1[:, :, 1].transpose(0, 2, 1),
                              a["f_w2"].transpose(0, 2, 1), b1], axis=2)
    arrays = {
        "x": a["x"].reshape(TOKENS, D),
        "wqkv": np.stack([a["wq"], a["wk"], a["wv"]], axis=1),
        "bq": a["bq"].reshape(D, 1), "bk": a["bk"].reshape(D, 1), "bv": a["bv"], "wo": a["wo"],
        "bo": a["bo"].reshape(1, D), "norm_scale": a["f_norm_scale"].reshape(D, 1),
        "gate_wT": a["f_gate_w"].T, "gate_b": a["f_gate_b"], "experts": experts, "b2": a["f_b2"],
    }
    arrays = {n: np.ascontiguousarray(v) for n, v in arrays.items()}
    nc = bacc.Bacc("TRN2", target_bir_lowering=False, num_devices=1)
    args = [nc.dram_tensor(n, v.shape, mybir.dt.from_np(v.dtype), kind="ExternalInput").ap() for n, v in arrays.items()]
    out = nc.dram_tensor("out", (TOKENS, D), F32, kind="ExternalOutput").ap()
    layer(nc, *args, out)
    r = run_bass_kernel_spmd(nc, [arrays], core_ids=[0])
    return r.results[0]["out"].reshape(BATCHES, SEQ, D)
```

```python
from contextlib import ExitStack

import concourse.bass as bass
from concourse import mybir

F32 = mybir.dt.float32
BF16 = mybir.dt.bfloat16
I32 = mybir.dt.int32
U32 = mybir.dt.uint32
ALU = mybir.AluOpType
ACT = mybir.ActivationFunctionType
AX = mybir.AxisListType

P = 128
D = 128
BATCHES = 4
SEQ = 1024
TOKENS = BATCHES * SEQ
TILES = TOKENS // P
BT = SEQ // P
E = 32
K = 4
CAP = TOKENS + P
SLOT_TILES = 160
ROW = D + 2
DEST, WEIGHT = D, D + 1
NOWHERE = 1 << 20
DUMMY = E * CAP
WCOLS = 3 * D + 2
U = 10
SCALE = float(D) ** -0.5
MASKED = -1.0e9
LIMIT, ALPHA = 7.0, 1.702
EPS = 1e-5
SPREAD = K * BT
HALF = SPREAD // 2

ROUTE = 21
DLT, MEMBER, RANKS_READ, COMB = 1, 4, 6, 13
POS_AT = [17, 21]
RANK_STEP = 6
PADS = 8
PLAN = 15
PT_AT = [0, 2, 4, 6, 8, 9, 10, 11, 12]


def layer(nc, x, wqkv, bq, bk, bv, wo, bo, norm_scale, gate_wT, gate_b, experts, b2, out):
    slots = nc.dram_tensor("slots", [DUMMY + P, ROW], F32).ap()
    parts = nc.dram_tensor("parts", [TOKENS * K, D], F32).ap()
    plan_dram = nc.dram_tensor("plan", [2 * P, 2], I32).ap()

    ctx = ExitStack()
    with ctx:
        def sb(name, shape, dt=F32):
            return ctx.enter_context(nc.sbuf_tensor(name, shape, dt))

        def sem(name):
            return ctx.enter_context(nc.semaphore(name))

        xs = sb("xs", [P, TILES, D])
        wqkv_s = sb("wqkv_s", [P, 3, D])
        wo_s = sb("wo_s", [P, D])
        bias_s = sb("bias_s", [P, 3])
        bq_scaled = sb("bq_scaled", [P, 1])
        bv_b = sb("bv_b", [P, D])
        scale_b = sb("scale_b", [P, D])
        gate_b_b = sb("gate_b_b", [P, E])
        gate_raw = sb("gate_raw", [P, E])
        gate_s = sb("gate_s", [P, E])
        b2_s = sb("b2_s", [E + 1, D])
        ident = sb("ident", [P, P])
        earlier = sb("earlier", [P, P], BF16)
        ones_bf = sb("ones_bf", [P, P], BF16)
        ones2 = sb("ones2", [P, 2])
        iota_e = sb("iota_e", [P, E])
        iota_i = sb("iota_i", [P, E], I32)
        cap_mask = sb("cap_mask", [P, 2 * P])
        extra = sb("extra", [P, 1])
        id_i = sb("id_i", [P, SPREAD], I32)
        ids = sb("ids", [P, SPREAD])
        tile_no_i = sb("tile_no_i", [P, 2], I32)
        tile_no = sb("tile_no", [P, 2])
        pad_rows = sb("pad_rows", [P, ROW])

        bnst = sb("bnst", [P, BT, 6])
        mv = sb("mv", [P, TILES, 2])
        stat = sb("stat", [P, 3, TILES])
        nv = sb("nv", [P, 2, TILES])
        nh = sb("nh", [P, TILES])
        nu = sb("nu", [P, TILES])
        nbits = sb("nbits", [P, TILES], I32)
        st_b = sb("st_b", [P, 3, BT])

        xn = sb("xn", [P, BT, D])
        tt = sb("tt", [P, BT, D])
        xnT = sb("xnT", [P, SEQ])
        qT = sb("qT", [P, SEQ])
        kT = sb("kT", [P, SEQ])
        v = sb("v", [P, BT, D])
        lg = sb("lg", [P, BT, E])
        mx = sb("mx", [P, BT, 8])
        mi = sb("mi", [P, BT, 8], U32)
        dlt = sb("dlt", [P, BT, K])
        ex = sb("ex", [P, BT, K])
        esum = sb("esum", [P, BT])
        erec = sb("erec", [P, BT])
        wk = sb("wk", [P, BT, K])
        idxf = sb("idxf", [P, BT, K])
        onehot = sb("onehot", [P, SPREAD, E])
        cw = sb("cw", [P, SPREAD, E])
        member = sb("member", [P, BT, E], BF16)
        seen = sb("seen", [P, E], BF16)
        seen_add = sb("seen_add", [P, E])
        comb = sb("comb", [P, BT, P])
        combT = sb("combT", [E + 1, SEQ])
        rank = sb("rank", [P, SPREAD])
        pos = sb("pos", [P, SPREAD], U32)
        pay = sb("pay", [P, SPREAD, ROW])

        prob = sb("prob", [P, 2, SEQ])
        probT = sb("probT", [P, 2, SEQ])
        neg_m = sb("neg_m", [P, BT])
        rsum = sb("rsum", [P, BT])
        rden = sb("rden", [P, BT])
        oT = sb("oT", [P, 2, P])

        cnt = sb("cnt", [P, E])
        nt_i = sb("nt_i", [P, E], I32)
        nt_s = sb("nt_s", [P, E], I32)
        nt = sb("nt", [P, E])
        ct = sb("ct", [P, E])
        one_row = sb("one_row", [P, E])
        ge = sb("ge", [P, 2, E])
        gt = sb("gt", [P, 2, E])
        eidx = sb("eidx", [P, 2])
        excl = sb("excl", [P, 2])
        loc = sb("loc", [P, 2])
        row_f = sb("row_f", [P, 2])
        plan = sb("plan_s", [P, 2, 2], I32)
        plan_row = sb("plan_row", [1, 4 * P], I32)
        pad_at = sb("pad_at", [P, E], I32)

        wx = sb("wx", [P, U, WCOLS])
        xg = sb("xg", [P, U, ROW])
        xgT = sb("xgT", [P, 2, P])
        hg = sb("hg", [P, 2, P])
        hl = sb("hl", [P, 2, P])
        hl1 = sb("hl1", [P, 2, P])
        sl = sb("sl", [P, 2, P])
        hw = sb("hw", [P, 2, P])
        ye = sb("ye", [P, U, D])
        CH = 4
        LB = 4
        yl = sb("yl", [P, LB, CH, K, D])
        ya = sb("ya", [P, 2, CH, 2, D])
        yb = sb("yb", [P, 2, CH, D])

        big = ctx.enter_context(nc.psum_tensor("big", [P, 2, 1024], F32))
        mid = ctx.enter_context(nc.psum_tensor("mid", [P, 2, 512], F32))
        o_ps_t = ctx.enter_context(nc.psum_tensor("o_ps_t", [P, 512], F32))
        rt_ps_t = ctx.enter_context(nc.psum_tensor("rt_ps_t", [P, 512], F32))
        lg_ps_v = rt_ps_t[:, 0:BT * E].rearrange("p (j e) -> p j e", e=E)
        rank_ps_v = rt_ps_t[:, 256:256 + BT * E].rearrange("p (j e) -> p j e", e=E)

        x_loaded = [sem(f"x_loaded{b}") for b in range(BATCHES)]
        const_loaded = sem("const_loaded")
        pool_const = sem("pool_const")
        dve_const = sem("dve_const")
        stats = sem("stats")
        xn_done, t_done, base_done, st_done = sem("xn_done"), sem("t_done"), sem("base_done"), sem("st_done")
        lg_done, top_done, route = sem("lg_done"), sem("top_done"), sem("route")
        v_done, masked, smax, ot_done = sem("v_done"), sem("masked"), sem("smax"), sem("ot_done")
        den_done, acc_done, b2_added = sem("den_done"), sem("acc_done"), sem("b2_added")
        xnT_ps, lg_ps, proj_ps, rank_ps = sem("xnT_ps"), sem("lg_ps"), sem("proj_ps"), sem("rank_ps")
        s_ps, pt_ps, o_ps, pr_ps = sem("s_ps"), sem("pt_ps"), sem("o_ps"), sem("pr_ps")
        ct_ps, b2_ps, cnt_ps = sem("ct_ps"), sem("b2_ps"), sem("cnt_ps")
        xnT_done, qk_done, ex_done, pay_done = sem("xnT_done"), sem("qk_done"), sem("ex_done"), sem("pay_done")
        p_done, pt_done, ct_done = sem("p_done"), sem("pt_done"), sem("ct_done")
        pay_free = sem("pay_free")
        pool_go, dve_go = sem("pool_go"), sem("dve_go")
        scattered = [sem(f"scattered{g}") for g in range(2)]
        planned, plan_out, plan_back = sem("planned"), sem("plan_out"), sem("plan_back")
        padded = sem("padded")
        tile_in = [sem(f"tile_in{u}") for u in range(U)]
        xg_ps, xg_done, h_ps, g_done = sem("xg_ps"), sem("xg_done"), sem("h_ps"), sem("g_done")
        l_done, sl_done, hw_done = sem("l_done"), sem("sl_done"), sem("hw_done")
        y_ps, y_done = sem("y_ps"), sem("y_done")
        returned = [sem(f"returned{u}") for u in range(U)]
        sum_in = [sem(f"sum_in{b}") for b in range(LB)]
        summed, stored = sem("summed"), sem("stored")

        NCONST = 11

        block = ctx.enter_context(nc.Block())

        def head_start(eng, *sems):
            for s in sems:
                eng.sem_inc(s, 1)

        def upto(eng, s, n):
            if not isinstance(n, int) or n > 0:
                eng.wait_ge(s, n + 1)

        def bcast(ap, shape):
            return ap.broadcast_to(shape)

        @block.sync
        def _(sp):
            x_v = x.rearrange("(i p) d -> p i d", p=P)
            sp.dma_start(xs[:, 0:BT, :], x_v[:, 0:BT, :]).then_inc(x_loaded[0], 16)
            sp.dma_start(wqkv_s[:], wqkv).then_inc(const_loaded, 16)
            sp.dma_start(bias_s[:, 0:1], bq).then_inc(const_loaded, 16)
            sp.dma_start(bias_s[:, 1:2], bk).then_inc(const_loaded, 16)
            sp.dma_start(bias_s[:, 2:3], norm_scale).then_inc(const_loaded, 16)
            sp.dma_start(gate_raw[:], gate_wT).then_inc(const_loaded, 16)
            sp.dma_start(gate_b_b[:], gate_b.partition_broadcast(P)).then_inc(const_loaded, 16)
            sp.dma_start(scale_b[:], norm_scale.rearrange("d a -> (d a)").partition_broadcast(P)).then_inc(const_loaded, 16)
            sp.dma_start(bv_b[:], bv.partition_broadcast(P)).then_inc(const_loaded, 16)
            sp.dma_start(wo_s[:], wo).then_inc(const_loaded, 16)
            sp.dma_start(b2_s[0:E, :], b2).then_inc(const_loaded, 16)
            sp.dma_start(b2_s[E:E + 1, :], bo).then_inc(const_loaded, 16)
            for b in range(1, BATCHES):
                sp.dma_start(xs[:, b * BT:(b + 1) * BT, :], x_v[:, b * BT:(b + 1) * BT, :]).then_inc(x_loaded[b], 16)

            for c in range(BATCHES - 1):
                for g in range(2):
                    sp.wait_ge(scattered[g], 16 * HALF * (c + 1))
                    sp.sem_inc(pay_free, 1)

            sp.wait_ge(planned, PLAN)
            sp.dma_start(plan_dram.rearrange("(q p) c -> p q c", p=P), plan[:]).then_inc(plan_out, 16)
            sp.wait_ge(pool_const, PAD_READY)
            sp.dma_start(slots[DUMMY:DUMMY + P, :], pad_rows[:]).then_inc(padded, 16)
            sp.wait_ge(plan_out, 16)
            sp.dma_start(plan_row[:], plan_dram.rearrange("(a n) c -> a (n c)", a=1)).then_inc(plan_back, 16)
            pad_reg = [sp.alloc_register(f"pad_reg{n}") for n in range(PADS)]
            with sp.Fori(0, E // PADS) as t:
                sp.reg_load(pad_reg, pad_at[0:1, bass.ds(t * PADS, PADS)])
                for r in pad_reg:
                    sp.dma_start(slots[bass.ds(sp.snap(r, min_val=0, max_val=DUMMY - P), P), :], pad_rows[:])\
                      .then_inc(padded, 16)
            sp.wait_ge(plan_back, 16)
            sp.wait_ge(padded, 16 * (E + 1))
            for g in range(2):
                sp.wait_ge(scattered[g], 16 * HALF * BATCHES)

            plan_reg = [sp.alloc_register(f"plan_reg{n}") for n in range(2 * U)]

            def load_turn(it, first):
                sp.reg_load(plan_reg, plan_row[0:1, bass.ds(it * (2 * U), 2 * U)])
                for u in range(U):
                    if not first:
                        sp.wait_ge(returned[u], 16 * it)
                    e = sp.snap(plan_reg[2 * u], min_val=0, max_val=E - 1)
                    at = sp.snap(plan_reg[2 * u + 1], min_val=0, max_val=DUMMY)
                    sp.dma_start(xg[:, u, :], slots[bass.ds(at, P), :]).then_inc(tile_in[u], 16)
                    sp.dma_start(wx[:, u, :], experts[bass.ds(e, 1), :, :].rearrange("a p n -> (a p) n"))\
                      .then_inc(tile_in[u], 16)

            load_turn(0, True)
            with sp.Fori(1, SLOT_TILES // U) as it:
                load_turn(it, False)
            for u in range(U):
                sp.wait_ge(returned[u], 16 * (SLOT_TILES // U))
            parts_v = parts.rearrange("(i p k) d -> p i (k d)", p=P, k=K)
            out_v = out.rearrange("(i p) d -> p i d", p=P)
            n_chunks = TILES // CH
            for q in range(n_chunks + LB - 1):
                if q < n_chunks:
                    if q >= LB:
                        sp.wait_ge(summed, 3 * (q - LB) + 1)
                    sp.dma_start(yl[:, q % LB].rearrange("p i k d -> p i (k d)"),
                                 parts_v[:, q * CH:(q + 1) * CH, :]).then_inc(sum_in[q % LB], 16)
                k = q - LB + 1
                if k >= 0:
                    sp.wait_ge(summed, 3 * k + 3)
                    sp.dma_start(out_v[:, k * CH:(k + 1) * CH, :], xs[:, k * CH:(k + 1) * CH, :]).then_inc(stored, 16)
            sp.wait_ge(stored, 16 * n_chunks)

        @block.gpsimd
        def _(pool):
            made = [0]

            def const(ins, then=True):
                made[0] += 1
                ins.then_inc(pool_const, 1)
                if then:
                    pool.wait_ge(pool_const, made[0])

            const(pool.memset(ident[:], 0.0))
            const(pool.affine_select(out=ident[:], in_=ident[:], compare_op=ALU.not_equal, fill=1.0, base=0,
                                     pattern=[[-1, P]], channel_multiplier=1), False)
            const(pool.memset(ones_bf[:], 1.0))
            const(pool.affine_select(out=earlier[:], in_=ones_bf[:], compare_op=ALU.is_gt, fill=0.0, base=0,
                                     pattern=[[1, P]], channel_multiplier=-1), False)
            const(pool.iota(iota_i[:], [[1, E]], base=0, channel_multiplier=0), False)
            const(pool.iota(id_i[:], [[K * P, BT], [1, K]], base=0, channel_multiplier=K), False)
            const(pool.iota(tile_no_i[:], [[P, 2]], base=0, channel_multiplier=1), False)
            const(pool.memset(cap_mask[:], 3.0e38))
            const(pool.affine_select(out=cap_mask[:], in_=cap_mask[:], compare_op=ALU.is_ge, fill=MASKED, base=-2,
                                     pattern=[[1, 2 * P]], channel_multiplier=-1), False)
            const(pool.memset(extra[:], float(SEQ - P)))
            const(pool.affine_select(out=extra[:], in_=extra[:], compare_op=ALU.is_ge, fill=0.0, base=-(P - 2),
                                     pattern=[[0, 1]], channel_multiplier=1), False)
            const(pool.memset(pad_rows[:], 0.0), False)
            const(pool.memset(one_row[:], 1.0))
            const(pool.iota(pad_rows[:, DEST:DEST + 1].bitcast(I32), [[0, 1]], base=NOWHERE, channel_multiplier=0))
            assert made[0] == PAD_READY

            slot_limit = pool.to_reg(DUMMY - 1)
            part_limit = pool.to_reg(TOKENS * K - 1)
            with pool.Fori(0, BATCHES) as c:
                for g in range(2):
                    upto(pool, pay_done, BT * c + 4 * g + 4)
                    pool.sem_inc(pool_go, 1)
                    upto(pool, route, ROUTE * c + POS_AT[g])
                    pool.sem_inc(pool_go, 1)
                    for n in range(HALF * g, HALF * g + HALF):
                        pool.indirect_dma_start(slots, bass.IndirectOffsetOnAxis(pos[:, n:n + 1], 0),
                                                pay[:, n, :], None, bounds_check=slot_limit, oob_is_err=False)\
                            .then_inc(scattered[g], 16)
            with pool.Fori(0, SLOT_TILES // U) as it:
                for u in range(U):
                    upto(pool, y_done, it * U + u + 1)
                    pool.sem_inc(pool_go, 1)
                    pool.indirect_dma_start(parts, bass.IndirectOffsetOnAxis(xg[:, u, DEST:DEST + 1].bitcast(U32), 0),
                                            ye[:, u, :], None, bounds_check=part_limit, oob_is_err=False)\
                        .then_inc(returned[u], 16)

        @block.tensor
        def _(pe):
            pe.wait_ge(const_loaded, 16 * NCONST)
            pe.wait_ge(pool_const, PAD_READY)
            pe.wait_ge(dve_const, DVE_CONST)

            head_start(pe, xnT_ps, lg_ps, proj_ps, rank_ps, s_ps, pt_ps, o_ps, pr_ps, ct_ps, b2_ps, xg_ps, h_ps, y_ps)

            def logits(r):
                upto(pe, pt_done, 12 * r - 12)
                upto(pe, v_done, 2 * r)
                for g in range(2):
                    upto(pe, xn_done, BT * r + 4 * (g + 1))
                    for j in range(4):
                        last = pe.transpose(mid[:, g, P * j:P * j + P], xn[:, 4 * g + j, :], ident[:])
                    last.then_inc(xnT_ps, 1)
                upto(pe, xnT_done, 2 * r + 2)
                upto(pe, acc_done, BT * r - BT)
                for j in range(BT):
                    last = pe.matmul(lg_ps_v[:, j, :], xnT[:, P * j:P * j + P], gate_s[:], start=True, stop=True)
                last.then_inc(lg_ps, 1)

            def ranks(r, busy):
                upto(pe, route, ROUTE * r + MEMBER)
                if busy is not None:
                    upto(pe, acc_done, busy)
                pe.matmul(rank_ps_v, ones_bf[:], bcast(seen[:].unsqueeze(1), [P, BT, E]), start=True, stop=False)
                for j in range(BT - 1):
                    pe.matmul(rank_ps_v[:, j + 1:BT, :], ones_bf[:],
                              bcast(member[:, j, :].unsqueeze(1), [P, BT - 1 - j, E]), start=False, stop=False)
                pe.matmul(rank_ps_v, earlier[:], member[:], start=False, stop=True).then_inc(rank_ps, 1)

            def expert_bias(r):
                upto(pe, p_done, BT * r)
                upto(pe, route, ROUTE * r + COMB)
                for j in range(BT):
                    last = pe.transpose(big[:, 0, P * j:P * j + P], comb[:, j, :], ident[:])
                    if j % 4 == 3:
                        last.then_inc(ct_ps, 1)
                upto(pe, ct_done, 2 * r + 2)
                for j in range(BT):
                    last = pe.matmul(big[:, 1, P * j:P * j + P], combT[:, P * j:P * j + P], b2_s[:],
                                     start=True, stop=True)
                last.then_inc(b2_ps, 1)

            def project_in(c):
                upto(pe, ct_done, 2 * c + 2)
                upto(pe, b2_added, c + 1)
                upto(pe, pt_done, 12 * c)
                for g in range(2):
                    for w in range(2):
                        pe.matmul(big[:, g, 512 * w:512 * w + 512], wqkv_s[:, w, :],
                                  xnT[:, 512 * g:512 * g + 512], start=True, stop=True).then_inc(proj_ps, 1)
                    for j in range(4):
                        last = pe.matmul(mid[:, g, P * j:P * j + P], xnT[:, P * (4 * g + j):P * (4 * g + j + 1)],
                                         wqkv_s[:, 2, :], start=True, stop=True)
                    last.then_inc(proj_ps, 1)

            def scores(c, i):
                w = SEQ - P * i
                if i < 2:
                    upto(pe, qk_done, 4 * c + 4)
                else:
                    upto(pe, p_done, BT * c + i - 1)
                for a in range(0, w, 512):
                    n = min(512, w - a)
                    last = pe.matmul(big[:, i % 2, a:a + n], qT[:, P * i:P * i + P],
                                     kT[:, P * i + a:P * i + a + n], start=True, stop=True)
                last.then_inc(s_ps, 1)

            def transpose_probs(c, i, xnT_out):
                upto(pe, p_done, BT * c + i + 1)
                if i == 0:
                    upto(pe, v_done, 2 * c + 2)
                    upto(pe, xnT_done, 2 * c + xnT_out)
                else:
                    upto(pe, pt_done, 12 * c + PT_AT[i])
                nb = BT - i
                for m in range((nb + 3) // 4):
                    for j in range(4 * m, min(nb, 4 * m + 4)):
                        last = pe.transpose(mid[:, m, P * (j % 4):P * (j % 4) + P],
                                            prob[:, i % 2, P * j:P * j + P], ident[:])
                    last.then_inc(pt_ps, 1)

            def values(c, i):
                upto(pe, pt_done, 12 * c + PT_AT[i + 1])
                upto(pe, ot_done, BT * c + i)
                o = o_ps_t[:, 0:P]
                nb = BT - i
                for j in range(nb):
                    last = pe.matmul(o, v[:, i + j, :], probT[:, i % 2, P * j:P * j + P],
                                     start=(j == 0), stop=(j == nb - 1 and i < BT - 1))
                if i == BT - 1:
                    for j in range(BT - 1):
                        last = pe.matmul(o[:, P - 2:P], v[:, j, :], ones2[:], start=False, stop=(j == BT - 2))
                last.then_inc(o_ps, 1)

            def project_out(c, i, rank_read):
                upto(pe, ot_done, BT * c + i + 1)
                upto(pe, acc_done, BT * c + i)
                if rank_read is not None:
                    upto(pe, route, rank_read)
                pe.matmul(rt_ps_t[:, 0:D], oT[:, i % 2, :], wo_s[:], start=True, stop=True).then_inc(pr_ps, 1)

            def attend(c, r):
                project_in(c)
                if r is not None:
                    logits(r)
                else:
                    upto(pe, route, ROUTE * BATCHES)
                    upto(pe, acc_done, BT * c)
                    pe.matmul(rt_ps_t[:, 0:E], ones_bf[:], seen[:], start=True, stop=True).then_inc(cnt_ps, 1)
                scores(c, 0)
                scores(c, 1)
                for i in range(BT + 2):
                    if i < BT:
                        transpose_probs(c, i, 2 if r is None else 4)
                    if i + 2 < BT:
                        scores(c, i + 2)
                    if i == RANK_STEP and r is not None:
                        ranks(r, BT * c + i - 2)
                    if 0 <= i - 1 < BT:
                        values(c, i - 1)
                    if 0 <= i - 2 < BT:
                        if i - 2 == 0:
                            if r is not None:
                                upto(pe, lg_done, BT * r + BT)
                            else:
                                pe.wait_ge(planned, 1)
                        project_out(c, i - 2, ROUTE * r + RANKS_READ if i == RANK_STEP and r is not None else None)
                if r is not None:
                    expert_bias(r)

            logits(0)
            ranks(0, None)
            expert_bias(0)
            with pe.Fori(0, BATCHES - 1) as c:
                attend(c, c + 1)
            attend(BATCHES - 1, None)

            def tile_T(it, u):
                n = it * U + u
                pe.wait_ge(tile_in[u], 32 * it + 32)
                upto(pe, xg_done, n - 1 if u >= 1 else it * U)
                pe.transpose(big[:, u % 2, 0:P], xg[:, u, 0:D], ident[:]).then_inc(xg_ps, 1)

            def tile_H(it, u):
                n = it * U + u
                upto(pe, xg_done, n + 1)
                upto(pe, l_done, 2 * n - 2 if u >= 1 else it * (2 * U))
                pe.matmul(big[:, u % 2, 512:512 + P], wx[:, u, 0:D], xgT[:, u % 2, :], start=True, stop=True)
                pe.matmul(big[:, u % 2, 512 + P:512 + 2 * P], wx[:, u, D:2 * D], xgT[:, u % 2, :],
                          start=True, stop=True).then_inc(h_ps, 1)

            def tile_Y(it, u):
                n = it * U + u
                upto(pe, hw_done, n + 1)
                upto(pe, y_done, n - 1 if u >= 1 else it * U)
                pe.matmul(mid[:, u % 2, 0:D], hw[:, u % 2, :], wx[:, u, 2 * D:3 * D],
                          start=True, stop=True).then_inc(y_ps, 1)

            upto(pe, p_done, BT * BATCHES)
            upto(pe, pt_done, 12 * BATCHES)
            turns = SLOT_TILES // U
            for u in range(3):
                tile_T(0, u)
                if u >= 1:
                    tile_H(0, u - 1)

            def turn(it, last):
                for u in range(U):
                    if not (last and u + 3 >= U):
                        tile_T(it + (u + 3) // U, (u + 3) % U)
                    if not (last and u + 2 >= U):
                        tile_H(it + (u + 2) // U, (u + 2) % U)
                    tile_Y(it, u)

            with pe.Fori(0, turns - 1) as it:
                turn(it, False)
            turn(turns - 1, True)

        @block.scalar
        def _(act):
            act.wait_ge(const_loaded, 16 * NCONST)
            act.wait_ge(dve_const, DVE_CONST)

            head_start(act, xnT_done, qk_done, ex_done, pay_done, p_done, pt_done, ct_done, xg_done, sl_done, y_done)

            def rows_T(r):
                for g in range(2):
                    upto(act, xnT_ps, 2 * r + g + 1)
                    act.copy(xnT[:, 512 * g:512 * g + 512], mid[:, g, :]).then_inc(xnT_done, 1)

            def payload(r, g, free):
                if free is not None:
                    act.wait_ge(pay_free, free)
                for j in range(4 * g, 4 * g + 4):
                    upto(act, t_done, BT * r + j + 1)
                    act.copy(pay[:, K * j:K * j + K, 0:D], bcast(tt[:, j, :].unsqueeze(1), [P, K, D]))\
                       .then_inc(pay_done, 1)

            def top_exp(r):
                upto(act, route, ROUTE * r + DLT)
                act.activation(ex[:], dlt[:], ACT.Exp).then_inc(ex_done, 1)

            def comb_T(r):
                for g in range(2):
                    upto(act, ct_ps, 2 * r + g + 1)
                    act.copy(combT[:, 512 * g:512 * g + 512], big[0:E + 1, 0, 512 * g:512 * g + 512])\
                       .then_inc(ct_done, 1)

            def qk(c, g, w):
                upto(act, proj_ps, 6 * c + 3 * g + w + 1)
                act.activation((qT, kT)[w][:, 512 * g:512 * g + 512], big[:, g, 512 * w:512 * w + 512], ACT.Identity,
                               bias=(bq_scaled[:, 0:1], bias_s[:, 1:2])[w], scale=(SCALE, 1.0)[w]).then_inc(qk_done, 1)

            def exps(c, i):
                upto(act, smax, BT * c + i + 1)
                upto(act, pt_ps, 12 * c + (PT_AT[i - 1] if i >= 2 else 0))
                w = SEQ - P * i
                act.activation(prob[:, i % 2, 0:w], big[:, i % 2, 0:w], ACT.Exp, bias=neg_m[:, i:i + 1],
                               accum_out=rsum[:, i:i + 1]).then_inc(p_done, 1)

            def probs_T(c, i):
                upto(act, o_ps, BT * c + max(i - 1, 0))
                nb = BT - i
                for m in range((nb + 3) // 4):
                    n = P * min(4, nb - 4 * m)
                    upto(act, pt_ps, 12 * c + PT_AT[i] + m + 1)
                    act.copy(probT[:, i % 2, 512 * m:512 * m + n], mid[:, m, 0:n]).then_inc(pt_done, 1)

            def attend(c, r):
                for g in range(2):
                    for w in range(2):
                        qk(c, g, w)
                if r is not None:
                    rows_T(r)
                exps(c, 0)
                for i in range(BT):
                    if i + 1 < BT:
                        exps(c, i + 1)
                    if r is not None:
                        if i == 4:
                            top_exp(r)
                        if i == 6:
                            payload(r, 0, 2 * c + 1)
                    probs_T(c, i)
                if r is not None:
                    comb_T(r)
                    payload(r, 1, 2 * c + 2)

            rows_T(0)
            top_exp(0)
            payload(0, 0, None)
            payload(0, 1, None)
            comb_T(0)
            with act.Fori(0, BATCHES - 1) as c:
                attend(c, c + 1)
            attend(BATCHES - 1, None)

            def tile_X(it, u):
                n = it * U + u
                upto(act, xg_ps, n + 1)
                upto(act, h_ps, n - 1 if u >= 1 else it * U)
                act.copy(xgT[:, u % 2, :], big[:, u % 2, 0:P]).then_inc(xg_done, 1)

            def tile_S(it, u):
                n = it * U + u
                upto(act, g_done, n + 1)
                upto(act, hw_done, n - 1 if u >= 1 else it * U)
                act.activation(sl[:, u % 2, :], hg[:, u % 2, :], ACT.Silu, scale=ALPHA).then_inc(sl_done, 1)

            def tile_E(it, u):
                n = it * U + u
                upto(act, y_ps, n + 1)
                act.activation(ye[:, u, :], mid[:, u % 2, 0:D], ACT.Copy, scale=xg[:, u, WEIGHT:WEIGHT + 1])\
                   .then_inc(y_done, 1)

            turns = SLOT_TILES // U
            for u in range(3):
                tile_X(0, u)
                if u >= 1:
                    tile_S(0, u - 1)

            def turn(it, last):
                for u in range(U):
                    if not (last and u + 3 >= U):
                        tile_X(it + (u + 3) // U, (u + 3) % U)
                    if not (last and u + 2 >= U):
                        tile_S(it + (u + 2) // U, (u + 2) % U)
                    tile_E(it, u)

            with act.Fori(0, turns - 1) as it:
                turn(it, False)
            turn(turns - 1, True)

        @block.vector
        def _(dve):
            n_const = [0]

            def const(ins):
                n_const[0] += 1
                ins.then_inc(dve_const, 1)

            dve.wait_ge(pool_const, PAD_READY)
            const(dve.tensor_copy(iota_e[:], iota_i[:]))
            const(dve.tensor_copy(ids[:], id_i[:]))
            const(dve.tensor_copy(tile_no[:], tile_no_i[:]))
            const(dve.memset(ones2[:], 1.0))
            const(dve.memset(seen[:], 0.0))
            const(dve.memset(comb[:], 0.0))
            dve.wait_ge(dve_const, n_const[0])
            const(dve.memset(comb[:, :, E:E + 1], 1.0))
            dve.wait_ge(const_loaded, 16 * NCONST)
            const(dve.tensor_scalar(bq_scaled[:], bias_s[:, 0:1], SCALE, None, ALU.mult))
            const(dve.tensor_scalar(gate_s[:], gate_raw[:], bias_s[:, 2:3], None, ALU.mult))
            assert n_const[0] == DVE_CONST

            n_stat = [0]

            def stat_step(ins, wait=True):
                n_stat[0] += 1
                ins.then_inc(stats, 1)
                if wait:
                    dve.wait_ge(stats, n_stat[0])

            def inv_sqrt(dst, a, cols):
                bits, half, t = nbits[:, cols], nh[:, cols], nv[:, 0, cols]
                stat_step(dve.tensor_scalar(bits, a.bitcast(I32), -0.5, float(0x5F3759DF), ALU.mult, ALU.add), False)
                stat_step(dve.tensor_scalar(half, a, -0.5, None, ALU.mult))
                guess = bits.bitcast(F32)
                for step in range(4):
                    stat_step(dve.tensor_tensor(t, guess, guess, ALU.mult))
                    stat_step(dve.tensor_tensor(t, t, half, ALU.mult))
                    stat_step(dve.scalar_tensor_tensor(dst, t, 1.5, guess, ALU.add, ALU.mult))
                    guess = dst

            def statistics(b0, b1):
                for b in range(b0, b1):
                    dve.wait_ge(x_loaded[b], 16)
                    for j in range(BT):
                        stat_step(dve.bn_stats(bnst[:, j, :], xs[:, b * BT + j, :]), j == BT - 1)
                    for j in range(BT):
                        stat_step(dve.bn_aggr(mv[:, b * BT + j, :], bnst[:, j, :]), j == BT - 1)
                cols = slice(b0 * BT, b1 * BT)
                a, var = nu[:, cols], mv[:, cols, 1]
                stat_step(dve.tensor_copy(stat[:, 0, cols], mv[:, cols, 0]), False)
                stat_step(dve.tensor_scalar(a, var, EPS, None, ALU.add))
                inv_sqrt(stat[:, 1, cols], a, cols)
                t = nv[:, 1, cols]
                stat_step(dve.tensor_tensor(t, stat[:, 1, cols], stat[:, 1, cols], ALU.mult))
                stat_step(dve.tensor_tensor(t, t, var, ALU.mult))
                stat_step(dve.tensor_scalar(a, t, EPS, None, ALU.add))
                inv_sqrt(stat[:, 2, cols], a, cols)

            head_start(dve, xn_done, t_done, base_done, st_done, lg_done, top_done, route, v_done, masked, smax,
                       ot_done, den_done, acc_done, b2_added, g_done, l_done, hw_done)

            def own(r, k):
                upto(dve, route, ROUTE * r + k)

            def normalise(r):
                dve.tensor_copy(st_b[:], stat[:, :, bass.ds(r * BT, BT)]).then_inc(st_done, 1)
                upto(dve, st_done, r + 1)
                for j in range(BT):
                    dve.tensor_scalar(xn[:, j, :], xs[:, bass.ds(r * BT + j, 1), :].rearrange("p a d -> p (a d)"),
                                      st_b[:, 0, j:j + 1], st_b[:, 1, j:j + 1], ALU.subtract, ALU.mult)\
                       .then_inc(xn_done, 1)

            def expert_rows(r):
                upto(dve, pay_done, BT * r)
                upto(dve, xn_done, BT * r + BT)
                for j in range(BT):
                    dve.scalar_tensor_tensor(tt[:, j, :], xn[:, j, :], st_b[:, 2, j:j + 1], scale_b[:],
                                             ALU.mult, ALU.mult).then_inc(t_done, 1)

            def start_output(r):
                rows = xs[:, bass.ds(r * BT, BT), :]
                dve.tensor_tensor(rows, rows, xn[:], ALU.add).then_inc(base_done, 1)

            def gate(r):
                upto(dve, lg_ps, r + 1)
                for j in range(BT):
                    dve.scalar_tensor_tensor(lg[:, j, :], lg_ps_v[:, j, :], st_b[:, 2, j:j + 1], gate_b_b[:],
                                             ALU.mult, ALU.add).then_inc(lg_done, 1)

            def top(r):
                upto(dve, lg_done, BT * r + BT)
                dve.sem_inc(dve_go, 1)
                for j in range(BT):
                    dve.max(mx[:, j, :], lg[:, j, :]).then_inc(top_done, 1)

            def top_index(r):
                upto(dve, top_done, 2 * BT * r + BT)
                dve.sem_inc(dve_go, 1)
                for j in range(BT):
                    dve.max_index(mi[:, j, :], mx[:, j, :], lg[:, j, :]).then_inc(top_done, 1)
                dve.tensor_tensor(dlt[:], mx[:, :, 0:K], bcast(mx[:, :, 0:1], [P, BT, K]), ALU.subtract)\
                   .then_inc(route, 1)
                upto(dve, top_done, 2 * BT * r + 2 * BT)
                dve.tensor_copy(idxf[:], mi[:, :, 0:K]).then_inc(route, 1)

            def one_hot(r):
                own(r, 2)
                dve.tensor_tensor(onehot[:], bcast(iota_e[:].unsqueeze(1), [P, SPREAD, E]),
                                  bcast(idxf[:].rearrange("p j k -> p (j k)").unsqueeze(2), [P, SPREAD, E]),
                                  ALU.is_equal).then_inc(route, 1)

            def members(r):
                own(r, 3)
                with nc.allow_low_precision(reason="zeros and ones are exact"):
                    dve.tensor_reduce(member[:], onehot[:].rearrange("p (j k) e -> p j e k", k=K), AX.X, ALU.add)\
                       .then_inc(route, 1)

            def members_sum(r):
                own(r, 4)
                dve.tensor_reduce(seen_add[:], member[:].rearrange("p j e -> p e j"), AX.X, ALU.add)\
                   .then_inc(route, 1)

            def slot_ranks(r):
                own(r, 5)
                upto(dve, rank_ps, r + 1)
                dve.tensor_tensor(cw[:].rearrange("p (j k) e -> p j k e", k=K),
                                  onehot[:].rearrange("p (j k) e -> p j k e", k=K),
                                  bcast(rank_ps_v.unsqueeze(2), [P, BT, K, E]), ALU.mult).then_inc(route, 1)
                dve.tensor_tensor(seen[:], seen[:], seen_add[:], ALU.add).then_inc(route, 1)
                own(r, 6)
                dve.tensor_reduce(rank[:], cw[:], AX.X, ALU.add).then_inc(route, 1)

            def weights(r):
                upto(dve, ex_done, r + 1)
                dve.tensor_reduce(esum[:], ex[:], AX.X, ALU.add).then_inc(route, 1)
                own(r, 9)
                dve.reciprocal(erec[:], esum[:]).then_inc(route, 1)
                own(r, 10)
                dve.tensor_tensor(wk[:], ex[:], bcast(erec[:].unsqueeze(2), [P, BT, K]), ALU.mult)\
                   .then_inc(route, 1)

            def combine(r):
                own(r, 11)
                dve.tensor_tensor(cw[:], onehot[:], bcast(wk[:].rearrange("p j k -> p (j k)").unsqueeze(2),
                                                          [P, SPREAD, E]), ALU.mult).then_inc(route, 1)
                own(r, 12)
                dve.tensor_reduce(comb[:, :, 0:E], cw[:].rearrange("p (j k) e -> p j e k", k=K), AX.X, ALU.add)\
                   .then_inc(route, 1)

            def address(r, g, free):
                n = slice(HALF * g, HALF * g + HALF)
                if free is not None:
                    dve.wait_ge(pay_free, free)
                dve.tensor_scalar(pay[:, n, WEIGHT:WEIGHT + 1],
                                  wk[:].rearrange("p j k -> p (j k)")[:, n].unsqueeze(2), 1.0 / ALPHA, None, ALU.mult)\
                   .then_inc(route, 1)
                dve.tensor_copy(pay[:, n, DEST:DEST + 1].bitcast(I32), ids[:, n].unsqueeze(2))\
                   .then_inc(route, 1)
                own(r, 15 + 4 * g)
                dve.tensor_scalar(ids[:, n], ids[:, n], float(K * SEQ), None, ALU.add).then_inc(route, 1)
                dve.scalar_tensor_tensor(pos[:, n], idxf[:].rearrange("p j k -> p (j k)")[:, n], float(CAP),
                                         rank[:, n], ALU.mult, ALU.add).then_inc(route, 1)

            def add_bias(r):
                upto(dve, b2_ps, r + 1)
                upto(dve, base_done, r + 1)
                rows = xs[:, bass.ds(r * BT, BT), :]
                dve.tensor_tensor(rows, rows, big[:, 1, :].rearrange("p (j d) -> p j d", d=D), ALU.add)\
                   .then_inc(b2_added, 1)

            def mask_max(c, i):
                w = SEQ - P * i
                wm = min(w, 2 * P)
                upto(dve, s_ps, BT * c + i + 1)
                dve.tensor_tensor(big[:, i % 2, 0:wm], big[:, i % 2, 0:wm], cap_mask[:, 0:wm], ALU.min)\
                   .then_inc(masked, 1)
                upto(dve, masked, BT * c + i + 1)
                dve.tensor_reduce(neg_m[:, i:i + 1], big[:, i % 2, 0:w], AX.X, ALU.max, negate=True).then_inc(smax, 1)

            def values_T(c, k):
                upto(dve, o_ps, BT * c + k + 1)
                dve.tensor_copy(oT[:, k % 2, :], o_ps_t[:, 0:P]).then_inc(ot_done, 1)

            def add_attention(c, k):
                if k == 0:
                    upto(dve, b2_added, c + 1)
                if k == BT - 1:
                    dve.tensor_tensor(rsum[:, k:k + 1], rsum[:, k:k + 1], extra[:], ALU.add).then_inc(den_done, 1)
                    upto(dve, den_done, (BT + 1) * c + BT)
                dve.reciprocal(rden[:, k:k + 1], rsum[:, k:k + 1]).then_inc(den_done, 1)
                upto(dve, den_done, (BT + 1) * c + k + (2 if k == BT - 1 else 1))
                upto(dve, pr_ps, BT * c + k + 1)
                row = xs[:, bass.ds(c * BT + k, 1), :].rearrange("p a d -> p (a d)")
                dve.scalar_tensor_tensor(row, rt_ps_t[:, 0:D], rden[:, k:k + 1], row, ALU.mult, ALU.add)\
                   .then_inc(acc_done, 1)

            def attend(c, r):
                if r is not None:
                    normalise(r)
                for g in range(2):
                    upto(dve, proj_ps, 6 * c + 3 * g + 3)
                    dve.tensor_tensor(v[:, 4 * g:4 * g + 4, :], mid[:, g, :].rearrange("p (j d) -> p j d", d=D),
                                      bcast(bv_b[:].unsqueeze(1), [P, 4, D]), ALU.add).then_inc(v_done, 1)
                if r is not None:
                    expert_rows(r)
                else:
                    make_plan()
                between = {} if r is None else {
                    0: [gate], 1: [top], 2: [top_index], 3: [one_hot], 4: [members], 5: [members_sum, start_output],
                    6: [slot_ranks], 7: [weights, combine], 8: [], 9: []}
                mask_max(c, 0)
                mask_max(c, 1)
                for i in range(BT + 2):
                    if i + 2 < BT:
                        mask_max(c, i + 2)
                    for step in between.get(i, []):
                        step(r)
                    if 0 <= i - 1 < BT:
                        values_T(c, i - 1)
                    if 0 <= i - 2 < BT:
                        add_attention(c, i - 2)
                if r is not None:
                    address(r, 0, 2 * c + 1)
                    add_bias(r)
                    address(r, 1, 2 * c + 2)

            n_plan = [0]

            def plan_step(ins):
                n_plan[0] += 1
                ins.then_inc(planned, 1)
                dve.wait_ge(planned, n_plan[0])

            def make_plan():
                dve.wait_ge(cnt_ps, 1)
                plan_step(dve.tensor_copy(cnt[:], rt_ps_t[:, 0:E]))
                plan_step(dve.tensor_scalar(nt_i[:], cnt[:], float(P - 1), None, ALU.add))
                plan_step(dve.tensor_scalar(nt_s[:], nt_i[:], 7, None, ALU.logical_shift_right))
                plan_step(dve.tensor_copy(nt[:], nt_s[:]))
                plan_step(dve.tensor_tensor_scan(ct[:], one_row[:], nt[:], 0.0, ALU.mult, ALU.add))
                plan_step(dve.tensor_tensor(ge[:], bcast(ct[:].unsqueeze(1), [P, 2, E]),
                                            bcast(tile_no[:].unsqueeze(2), [P, 2, E]), ALU.is_le))
                plan_step(dve.tensor_reduce(eidx[:], ge[:], AX.X, ALU.add))
                plan_step(dve.tensor_tensor(gt[:], ge[:], bcast(nt[:].unsqueeze(1), [P, 2, E]), ALU.mult))
                plan_step(dve.tensor_reduce(excl[:], gt[:], AX.X, ALU.add))
                plan_step(dve.tensor_tensor(loc[:], tile_no[:], excl[:], ALU.subtract))
                plan_step(dve.tensor_scalar(row_f[:], eidx[:], float(CAP), None, ALU.mult))
                plan_step(dve.scalar_tensor_tensor(loc[:], loc[:], float(P), row_f[:], ALU.mult, ALU.add))
                plan_step(dve.tensor_scalar(plan[:, :, 0], eidx[:], float(E - 1), None, ALU.min))
                plan_step(dve.tensor_scalar(plan[:, :, 1], loc[:], float(DUMMY), None, ALU.min))
                plan_step(dve.scalar_tensor_tensor(pad_at[:], iota_e[:], float(CAP), cnt[:], ALU.mult, ALU.add))
                assert n_plan[0] == PLAN

            statistics(0, 1)
            normalise(0)
            expert_rows(0)
            for step in (gate, top, top_index, one_hot, members, members_sum, slot_ranks, weights, combine):
                step(0)
            address(0, 0, None)
            address(0, 1, None)
            start_output(0)
            add_bias(0)
            statistics(1, BATCHES)
            with dve.Fori(0, BATCHES - 1) as c:
                attend(c, c + 1)
            attend(BATCHES - 1, None)

            def tile_HW(it, u):
                n = it * U + u
                upto(dve, sl_done, n + 1)
                upto(dve, l_done, 2 * n + 2)
                upto(dve, y_ps, n - 1 if u >= 1 else it * U)
                dve.tensor_tensor(hw[:, u % 2, :], hl1[:, u % 2, :], sl[:, u % 2, :], ALU.mult).then_inc(hw_done, 1)

            def tile_G(it, u):
                n = it * U + u
                upto(dve, h_ps, n + 1)
                upto(dve, sl_done, n - 1 if u >= 1 else it * U)
                dve.tensor_scalar(hg[:, u % 2, :], big[:, u % 2, 512:512 + P], wx[:, u, 3 * D:3 * D + 1], LIMIT,
                                  ALU.add, ALU.min).then_inc(g_done, 1)
                dve.tensor_scalar(hl[:, u % 2, :], big[:, u % 2, 512 + P:512 + 2 * P], wx[:, u, 3 * D + 1:3 * D + 2],
                                  LIMIT, ALU.add, ALU.min).then_inc(l_done, 1)
                upto(dve, l_done, 2 * n + 1)
                dve.tensor_scalar(hl1[:, u % 2, :], hl[:, u % 2, :], -LIMIT, 1.0, ALU.max, ALU.add).then_inc(l_done, 1)

            turns = SLOT_TILES // U
            for u in range(2):
                tile_G(0, u)

            def turn(it, last):
                for u in range(U):
                    tile_HW(it, u)
                    if not (last and u + 2 >= U):
                        tile_G(it + (u + 2) // U, (u + 2) % U)

            with dve.Fori(0, turns - 1) as it:
                turn(it, False)
            turn(turns - 1, True)

            for q in range(TILES // CH):
                dve.wait_ge(sum_in[q % LB], 16 * (q // LB + 1))
                y = yl[:, q % LB]
                dve.tensor_tensor(ya[:, q % 2], y[:, :, 0:2, :], y[:, :, 2:4, :], ALU.add).then_inc(summed, 1)
                dve.wait_ge(summed, 3 * q + 1)
                dve.tensor_tensor(yb[:, q % 2], ya[:, q % 2, :, 0, :], ya[:, q % 2, :, 1, :], ALU.add).then_inc(summed, 1)
                dve.wait_ge(summed, 3 * q + 2)
                rows = xs[:, q * CH:(q + 1) * CH, :]
                dve.tensor_tensor(rows, rows, yb[:, q % 2], ALU.add).then_inc(summed, 1)
                dve.wait_ge(summed, 3 * q + 3)


PAD_READY = 14
DVE_CONST = 9


def kernel(**inputs):
    import numpy as np
    import concourse.bacc as bacc
    from concourse.bass_utils import run_bass_kernel_spmd

    a = {n.replace("L0_attn_", "").replace("L0_ffn_", "f_"): np.asarray(v) for n, v in inputs.items()}
    w1 = a["f_w1"].reshape(E, D, 2, D)
    b1 = a["f_b1"].reshape(E, D, 2)
    experts = np.concatenate([w1[:, :, 0].transpose(0, 2, 1), w1[:, :, 1].transpose(0, 2, 1),
                              a["f_w2"].transpose(0, 2, 1), b1], axis=2)
    arrays = {
        "x": a["x"].reshape(TOKENS, D),
        "wqkv": np.stack([a["wq"], a["wk"], a["wv"]], axis=1),
        "bq": a["bq"].reshape(D, 1), "bk": a["bk"].reshape(D, 1), "bv": a["bv"], "wo": a["wo"],
        "bo": a["bo"].reshape(1, D), "norm_scale": a["f_norm_scale"].reshape(D, 1),
        "gate_wT": a["f_gate_w"].T, "gate_b": a["f_gate_b"], "experts": experts, "b2": a["f_b2"],
    }
    arrays = {n: np.ascontiguousarray(v) for n, v in arrays.items()}
    nc = bacc.Bacc("TRN2", target_bir_lowering=False, num_devices=1)
    args = [nc.dram_tensor(n, v.shape, mybir.dt.from_np(v.dtype), kind="ExternalInput").ap() for n, v in arrays.items()]
    out = nc.dram_tensor("out", (TOKENS, D), F32, kind="ExternalOutput").ap()
    layer(nc, *args, out)
    r = run_bass_kernel_spmd(nc, [arrays], core_ids=[0])
    return r.results[0]["out"].reshape(BATCHES, SEQ, D)
```

```python
from contextlib import ExitStack

import concourse.bass as bass
from concourse import mybir

F32 = mybir.dt.float32
BF16 = mybir.dt.bfloat16
I32 = mybir.dt.int32
U32 = mybir.dt.uint32
ALU = mybir.AluOpType
ACT = mybir.ActivationFunctionType
AX = mybir.AxisListType

P = 128
D = 128
BATCHES = 4
SEQ = 1024
TOKENS = BATCHES * SEQ
TILES = TOKENS // P
BT = SEQ // P
E = 32
K = 4
CAP = TOKENS + P
SLOT_TILES = 160
ROW = D + 2
DEST, WEIGHT = D, D + 1
NOWHERE = 1 << 20
DUMMY = E * CAP
WCOLS = 3 * D + 2
ACT_SLOTS = range(2, 15)
LAG = 5
EARLY = 14
AHEAD = 5
U = 20
SCALE = float(D) ** -0.5
MASKED = -1.0e9
UNSEEN = -1.0e30
LIMIT, ALPHA = 7.0, 1.702
EPS = 1e-5
SPREAD = K * BT
HALF = SPREAD // 2

ROUTE = 23
DLT, MEMBER, RANKS_READ, SEEN, COMB = 2, 6, 8, 9, 23
POS_AT = [17, 21]
PADS = 8
PLAN = 15
PT_AT = [0, 2, 4, 6, 8, 9, 10, 11, 12]


def layer(nc, x, wqkv, bq, bk, bv, wo, bo, norm_scale, gate_wT, gate_b, experts, b2, out):
    slots = nc.dram_tensor("slots", [DUMMY + P, ROW], F32).ap()
    parts = nc.dram_tensor("parts", [TOKENS * K, D], F32).ap()
    plan_dram = nc.dram_tensor("plan", [2 * P, 2], I32).ap()

    ctx = ExitStack()
    with ctx:
        def sb(name, shape, dt=F32):
            return ctx.enter_context(nc.sbuf_tensor(name, shape, dt))

        def sem(name):
            return ctx.enter_context(nc.semaphore(name))

        xs = sb("xs", [P, TILES, D])
        wqkv_s = sb("wqkv_s", [P, 3, D])
        wo_s = sb("wo_s", [P, D])
        wvo_s = sb("wvo_s", [P, D])
        bias_s = sb("bias_s", [P, 4])
        bv_last = sb("bv_last", [P, E + 1])
        bq_scaled = sb("bq_scaled", [P, 1])
        gate_b_b = sb("gate_b_b", [P, E])
        gate_raw = sb("gate_raw", [P, E])
        gate_s = sb("gate_s", [P, E])
        b2_s = sb("b2_s", [E + 1, D])
        ident = sb("ident", [P, P])
        earlier = sb("earlier", [P, P], BF16)
        ones_bf = sb("ones_bf", [P, P], BF16)
        ones2 = sb("ones2", [P, 2])
        iota_e = sb("iota_e", [P, E])
        iota_i = sb("iota_i", [P, E], I32)
        ident_bf = sb("ident_bf", [P, P], BF16)
        unseen = sb("unseen", [P, 2 * P], BF16)
        cap_mask = sb("cap_mask", [P, P])
        extra = sb("extra", [P, 1])
        id_i = sb("id_i", [P, SPREAD], I32)
        ids = sb("ids", [P, SPREAD])
        tile_no_i = sb("tile_no_i", [P, 2], I32)
        tile_no = sb("tile_no", [P, 2])
        pad_rows = sb("pad_rows", [P, ROW])

        bnst = sb("bnst", [P, BT, 6])
        mv = sb("mv", [P, TILES, 2])
        stat = sb("stat", [P, 3, TILES])
        nv = sb("nv", [P, 2, TILES])
        nh = sb("nh", [P, 2, TILES])
        nu = sb("nu", [P, 2, TILES])
        nbits = sb("nbits", [P, 2, TILES], I32)
        st_b = sb("st_b", [P, 3, BT])

        xn = sb("xn", [P, BT, D])
        tt = sb("tt", [P, BT, D])
        rs_b = sb("rs_b", [P, BT])
        xnT = sb("xnT", [P, SEQ])
        qT = sb("qT", [P, SEQ])
        kT = sb("kT", [P, SEQ])
        v = sb("v", [P, BT, D])
        lg = sb("lg", [P, BT, E])
        mx = sb("mx", [P, BT, 8])
        mi = sb("mi", [P, BT, 8], U32)
        dlt = sb("dlt", [P, BT, K])
        ex = sb("ex", [P, BT, K])
        esum = sb("esum", [P, BT])
        erec = sb("erec", [P, BT])
        wk = sb("wk", [P, BT, K])
        idxf = sb("idxf", [P, BT, K])
        elg = sb("elg", [P, BT, E])
        onehot = sb("onehot", [P, SPREAD, E], BF16)
        pairs = sb("pairs", [P, BT, 2, E], BF16)
        cw = sb("cw", [P, SPREAD, E])
        member = sb("member", [P, BT, E], BF16)
        seen = sb("seen", [P, E], BF16)
        seen_add = sb("seen_add", [P, E])
        comb = sb("comb", [P, BT, P])
        combT = sb("combT", [E + 1, SEQ])
        rank = sb("rank", [P, SPREAD])
        pos = sb("pos", [P, SPREAD], U32)
        pay = sb("pay", [P, SPREAD, ROW])

        prob = sb("prob", [P, 2, SEQ])
        probT = sb("probT", [P, 2, SEQ])
        neg_m = sb("neg_m", [P, BT])
        rsum = sb("rsum", [P, BT])
        rden = sb("rden", [P, BT])
        vs_pad = sb("vs_pad", [P, P])

        cnt = sb("cnt", [P, E])
        nt_i = sb("nt_i", [P, E], I32)
        nt_s = sb("nt_s", [P, E], I32)
        nt = sb("nt", [P, E])
        ct = sb("ct", [P, E])
        one_row = sb("one_row", [P, E])
        ge = sb("ge", [P, 2, E])
        gt = sb("gt", [P, 2, E])
        eidx = sb("eidx", [P, 2])
        excl = sb("excl", [P, 2])
        loc = sb("loc", [P, 2])
        row_f = sb("row_f", [P, 2])
        plan = sb("plan_s", [P, 2, 2], I32)
        plan_row = sb("plan_row", [1, 4 * P], I32)
        pad_at = sb("pad_at", [P, E], I32)

        wx = sb("wx", [P, U, WCOLS])
        xg = sb("xg", [P, U, ROW])
        xgT = sb("xgT", [P, 2, P])
        hg = sb("hg", [P, 2, P])
        hl = sb("hl", [P, 2, P])
        b1p = sb("b1p", [P, U])
        sl = sb("sl", [P, 2, P])
        hw = sb("hw", [P, 2, P])
        ye = sb("ye", [P, U, D])
        CH = 2
        LB = 8
        yl = sb("yl", [P, LB, CH, K, D])
        ya = sb("ya", [P, 2, CH, 2, D])
        yb = sb("yb", [P, 2, CH, D])

        big = ctx.enter_context(nc.psum_tensor("big", [P, 2, 1024], F32))
        mid = ctx.enter_context(nc.psum_tensor("mid", [P, 2, 512], F32))
        o_ps_t = ctx.enter_context(nc.psum_tensor("o_ps_t", [P, 512], F32))
        rt_ps_t = ctx.enter_context(nc.psum_tensor("rt_ps_t", [P, 512], F32))
        lg_ps_v = rt_ps_t[:, 0:BT * E].rearrange("p (j e) -> p j e", e=E)
        rank_ps_v = rt_ps_t[:, 256:256 + BT * E].rearrange("p (j e) -> p j e", e=E)

        x_loaded = [sem(f"x_loaded{b}") for b in range(BATCHES)]
        const_loaded = sem("const_loaded")
        pool_const = sem("pool_const")
        dve_const = sem("dve_const")
        stats = sem("stats")
        xn_done, rs_done, tt_done, base_done, st_done = sem("xn_done"), sem("rs_done"), sem("tt_done"), sem("base_done"), sem("st_done")
        lg_done, top_done, route = sem("lg_done"), sem("top_done"), sem("route")
        v_done, masked, smax, w_done = sem("v_done"), sem("masked"), sem("smax"), sem("w_done")
        den_done, acc_done, b2_added = sem("den_done"), sem("acc_done"), sem("b2_added")
        xnT_ps, lg_ps, qk_ps, v_ps, rank_ps = sem("xnT_ps"), sem("lg_ps"), sem("qk_ps"), sem("v_ps"), sem("rank_ps")
        s_ps, pt_ps, o_ps, vs_ps, w_ps = sem("s_ps"), sem("pt_ps"), sem("o_ps"), sem("vs_ps"), sem("w_ps")
        vs_done = sem("vs_done")
        ct_ps, b2_ps, cnt_ps = sem("ct_ps"), sem("b2_ps"), sem("cnt_ps")
        xnT_done, qk_done, ex_done, pay_done = sem("xnT_done"), sem("qk_done"), sem("ex_done"), sem("pay_done")
        p_done, pt_done, ct_done = sem("p_done"), sem("pt_done"), sem("ct_done")
        pay_free = sem("pay_free")
        pool_go, dve_go = sem("pool_go"), sem("dve_go")
        scattered = [sem(f"scattered{g}") for g in range(2)]
        planned, plan_out, plan_back = sem("planned"), sem("plan_out"), sem("plan_back")
        padded = sem("padded")
        rows_in = [sem(f"rows_in{u}") for u in range(U)]
        weights_in = [sem(f"weights_in{u}") for u in range(U)]
        xg_ps, xg_done, h_ps, g_done = sem("xg_ps"), sem("xg_done"), sem("h_ps"), sem("g_done")
        b1p_done, l_done, sl_done, hw_done = sem("b1p_done"), sem("l_done"), sem("sl_done"), sem("hw_done")
        y_ps, y_done = sem("y_ps"), sem("y_done")
        returned = [sem(f"returned{u}") for u in range(U)]
        sum_in = [sem(f"sum_in{b}") for b in range(LB)]
        summed, stored = sem("summed"), sem("stored")

        NCONST = 10

        block = ctx.enter_context(nc.Block())

        def head_start(eng, *sems):
            for s in sems:
                eng.sem_inc(s, 1)

        def upto(eng, s, n):
            if not isinstance(n, int) or n > 0:
                eng.wait_ge(s, n + 1)

        def bcast(ap, shape):
            return ap.broadcast_to(shape)

        @block.sync
        def _(sp):
            x_v = x.rearrange("(i p) d -> p i d", p=P)
            sp.dma_start(xs[:, 0:BT, :], x_v[:, 0:BT, :]).then_inc(x_loaded[0], 16)
            sp.dma_start(wqkv_s[:], wqkv).then_inc(const_loaded, 16)
            sp.dma_start(bias_s[:, 0:1], bq).then_inc(const_loaded, 16)
            sp.dma_start(bias_s[:, 1:2], bk).then_inc(const_loaded, 16)
            sp.dma_start(bias_s[:, 2:3], norm_scale).then_inc(const_loaded, 16)
            sp.dma_start(gate_raw[:], gate_wT).then_inc(const_loaded, 16)
            sp.dma_start(gate_b_b[:], gate_b.partition_broadcast(P)).then_inc(const_loaded, 16)
            sp.dma_start(bias_s[:, 3:4], bv).then_inc(const_loaded, 16)
            sp.dma_start(wo_s[:], wo).then_inc(const_loaded, 16)
            sp.dma_start(b2_s[0:E, :], b2).then_inc(const_loaded, 16)
            sp.dma_start(b2_s[E:E + 1, :], bo).then_inc(const_loaded, 16)
            sp.wait_ge(x_loaded[0], 16)
            for b in range(1, BATCHES):
                sp.dma_start(xs[:, b * BT:(b + 1) * BT, :], x_v[:, b * BT:(b + 1) * BT, :]).then_inc(x_loaded[b], 16)

            for c in range(BATCHES - 1):
                for g in range(2):
                    sp.wait_ge(scattered[g], 16 * HALF * (c + 1))
                    sp.sem_inc(pay_free, 1)

            sp.wait_ge(planned, PLAN)
            sp.dma_start(plan_dram.rearrange("(q p) c -> p q c", p=P), plan[:]).then_inc(plan_out, 16)
            sp.wait_ge(pool_const, PAD_READY)
            sp.dma_start(slots[DUMMY:DUMMY + P, :], pad_rows[:]).then_inc(padded, 16)
            pad_reg = [sp.alloc_register(f"pad_reg{n}") for n in range(PADS)]
            with sp.Fori(0, E // PADS) as t:
                sp.reg_load(pad_reg, pad_at[0:1, bass.ds(t * PADS, PADS)])
                for r in pad_reg:
                    sp.dma_start(slots[bass.ds(sp.snap(r, min_val=0, max_val=DUMMY - P), P), :], pad_rows[:])\
                      .then_inc(padded, 16)
            sp.wait_ge(plan_out, 16)
            sp.dma_start(plan_row[:], plan_dram.rearrange("(a n) c -> a (n c)", a=1)).then_inc(plan_back, 16)
            sp.wait_ge(plan_back, 16)
            sp.wait_ge(padded, 16 * (E + 1))
            plan_reg = [sp.alloc_register(f"plan_reg{n}") for n in range(2 * U)]

            def load_plan(first):
                for h in (0, U):
                    sp.reg_load(plan_reg[h:h + U], plan_row[0:1, bass.ds(first + h, U)])

            def load_weights(u):
                sp.dma_start(wx[:, u, :], experts[bass.ds(sp.snap(plan_reg[2 * u], min_val=0, max_val=E - 1), 1), :, :]
                             .rearrange("a p n -> (a p) n")).then_inc(weights_in[u], 16)

            def load_rows(u):
                sp.dma_start(xg[:, u, :], slots[bass.ds(sp.snap(plan_reg[2 * u + 1], min_val=0, max_val=DUMMY), P), :])\
                  .then_inc(rows_in[u], 16)

            load_plan(0)
            for u in range(EARLY):
                load_weights(u)
            for g in range(2):
                sp.wait_ge(scattered[g], 16 * HALF * BATCHES)
            for u in range(U):
                load_rows(u)
                if EARLY <= u + 4 < U:
                    load_weights(u + 4)
            with sp.Fori(1, SLOT_TILES // U) as it:
                load_plan(it * (2 * U))
                for u in range(U):
                    sp.wait_ge(returned[u], 16 * it)
                    if u not in ACT_SLOTS:
                        load_rows(u)
                    load_weights(u)
            for u in range(U):
                sp.wait_ge(returned[u], 16 * (SLOT_TILES // U))
            parts_v = parts.rearrange("(i p k) d -> p i (k d)", p=P, k=K)
            for q in range(TILES // CH):
                if q >= LB:
                    sp.wait_ge(summed, 3 * (q - LB) + 1)
                sp.dma_start(yl[:, q % LB].rearrange("p i k d -> p i (k d)"),
                             parts_v[:, q * CH:(q + 1) * CH, :]).then_inc(sum_in[q % LB], 16)

        @block.gpsimd
        def _(pool):
            made = [0]

            def const(ins, then=True):
                made[0] += 1
                ins.then_inc(pool_const, 1)
                if then:
                    pool.wait_ge(pool_const, made[0])

            const(pool.memset(ident[:], 0.0))
            const(pool.affine_select(out=ident[:], in_=ident[:], compare_op=ALU.not_equal, fill=1.0, base=0,
                                     pattern=[[-1, P]], channel_multiplier=1), False)
            const(pool.memset(ident_bf[:], 0.0))
            const(pool.affine_select(out=ident_bf[:], in_=ident_bf[:], compare_op=ALU.not_equal, fill=1.0, base=0,
                                     pattern=[[-1, P]], channel_multiplier=1), False)
            const(pool.memset(ones_bf[:], 1.0))
            const(pool.affine_select(out=earlier[:], in_=ones_bf[:], compare_op=ALU.is_gt, fill=0.0, base=0,
                                     pattern=[[1, P]], channel_multiplier=-1), False)
            const(pool.iota(iota_i[:], [[1, E]], base=0, channel_multiplier=0), False)
            const(pool.iota(id_i[:], [[K * P, BT], [1, K]], base=0, channel_multiplier=K), False)
            const(pool.iota(tile_no_i[:], [[P, 2]], base=0, channel_multiplier=1), False)
            const(pool.memset(cap_mask[:], 3.0e38))
            const(pool.affine_select(out=cap_mask[:], in_=cap_mask[:], compare_op=ALU.is_ge, fill=MASKED, base=-2,
                                     pattern=[[1, P]], channel_multiplier=-1), False)
            const(pool.memset(unseen[:], 0.0))
            const(pool.affine_select(out=unseen[:], in_=unseen[:], compare_op=ALU.is_ge, fill=UNSEEN, base=-2,
                                     pattern=[[1, 2 * P]], channel_multiplier=-1), False)
            const(pool.memset(vs_pad[:], 0.0), False)
            const(pool.memset(bv_last[:], 0.0), False)
            const(pool.memset(extra[:], float(SEQ - P)))
            const(pool.affine_select(out=extra[:], in_=extra[:], compare_op=ALU.is_ge, fill=0.0, base=-(P - 2),
                                     pattern=[[0, 1]], channel_multiplier=1), False)
            const(pool.memset(pad_rows[:], 0.0), False)
            const(pool.memset(one_row[:], 1.0))
            const(pool.iota(pad_rows[:, DEST:DEST + 1].bitcast(I32), [[0, 1]], base=NOWHERE, channel_multiplier=0))
            assert made[0] == PAD_READY

            slot_limit = pool.to_reg(DUMMY - 1)
            part_limit = pool.to_reg(TOKENS * K - 1)
            with pool.Fori(0, BATCHES) as c:
                for g in range(2):
                    upto(pool, pay_done, BT * c + 4 * g + 4)
                    pool.sem_inc(pool_go, 1)
                    upto(pool, route, ROUTE * c + POS_AT[g])
                    pool.sem_inc(pool_go, 1)
                    for n in range(HALF * g, HALF * g + HALF):
                        pool.indirect_dma_start(slots, bass.IndirectOffsetOnAxis(pos[:, n:n + 1], 0),
                                                pay[:, n, :], None, bounds_check=slot_limit, oob_is_err=False)\
                            .then_inc(scattered[g], 16)
            with pool.Fori(0, SLOT_TILES // U) as it:
                for u in range(U):
                    upto(pool, y_done, it * U + u + 1)
                    pool.sem_inc(pool_go, 1)
                    pool.indirect_dma_start(parts, bass.IndirectOffsetOnAxis(xg[:, u, DEST:DEST + 1].bitcast(U32), 0),
                                            ye[:, u, :], None, bounds_check=part_limit, oob_is_err=False)\
                        .then_inc(returned[u], 16)

        @block.tensor
        def _(pe):
            pe.wait_ge(pool_const, PAD_READY)

            head_start(pe, xnT_ps, lg_ps, qk_ps, v_ps, rank_ps, s_ps, pt_ps, o_ps, vs_ps, ct_ps, b2_ps, xg_ps, h_ps, y_ps)

            def rows_T(r, g):
                if g == 0:
                    upto(pe, route, ROUTE * r - ROUTE + RANKS_READ)
                else:
                    upto(pe, xnT_done, 2 * r + 1)
                upto(pe, xn_done, BT * r + 4 * (g + 1))
                for j in range(4):
                    last = pe.transpose(rt_ps_t[:, P * j:P * j + P], xn[:, 4 * g + j, :], ident[:])
                last.then_inc(xnT_ps, 1)

            def logits(r):
                upto(pe, xnT_done, 2 * r + 2)
                for j in range(BT):
                    last = pe.matmul(lg_ps_v[:, j, :], xnT[:, P * j:P * j + P], gate_s[:], start=True, stop=True)
                last.then_inc(lg_ps, 1)

            def ranks(r):
                upto(pe, route, ROUTE * r + MEMBER)
                pe.matmul(rank_ps_v, ones_bf[:], bcast(seen[:].unsqueeze(1), [P, BT, E]), start=True, stop=False)
                for j in range(BT - 1):
                    pe.matmul(rank_ps_v[:, j + 1:BT, :], ones_bf[:],
                              bcast(member[:, j, :].unsqueeze(1), [P, BT - 1 - j, E]), start=False, stop=False)
                pe.matmul(rank_ps_v, earlier[:], member[:], start=False, stop=True).then_inc(rank_ps, 1)

            def comb_T(c):
                upto(pe, route, ROUTE * c + COMB)
                for g in range(2):
                    upto(pe, p_done, BT * c + 3 + g)
                    for j in range(4):
                        last = pe.transpose(big[:, g, 512 + P * j:512 + P * j + P], comb[:, 4 * g + j, :], ident[:])
                    last.then_inc(ct_ps, 1)

            def expert_bias(c):
                for g in range(2):
                    upto(pe, ct_done, 2 * c + g + 1)
                    for j in range(4):
                        last = pe.matmul(big[:, g, 512 + P * j:512 + P * j + P],
                                         combT[:, P * (4 * g + j):P * (4 * g + j + 1)], b2_s[:], start=True, stop=True)
                    last.then_inc(b2_ps, 1)

            def project_qk(r, g):
                for w in range(2):
                    if g == 0:
                        upto(pe, b2_added, 2 * r - 1 + w)
                    else:
                        upto(pe, qk_done, 4 * r + 1 + w)
                    pe.matmul(big[:, w, 512:1024], wqkv_s[:, w, :], xnT[:, 512 * g:512 * g + 512],
                              start=True, stop=True).then_inc(qk_ps, 1)

            def project_v(r):
                for g in range(2):
                    upto(pe, pt_done, 12 * r - 12 + (PT_AT[4], 12)[g])
                    for j in range(4):
                        last = pe.matmul(mid[:, 1 - g, P * j:P * j + P],
                                         xnT[:, P * (4 * g + j):P * (4 * g + j + 1)], wvo_s[:],
                                         start=True, stop=True)
                    last.then_inc(v_ps, 1)

            def scores(c, i):
                w = SEQ - P * i
                if i < 2:
                    upto(pe, qk_done, 4 * c + 4)
                    upto(pe, p_done, BT * c)
                else:
                    upto(pe, p_done, BT * c + i - 1)
                for a in range(0, w, 512):
                    n = min(512, w - a)
                    last = pe.matmul(big[:, i % 2, a:a + n], qT[:, P * i:P * i + P],
                                     kT[:, P * i + a:P * i + a + n], start=True, stop=(a > 0 or i == BT - 1))
                if i < BT - 1:
                    last = pe.matmul(big[:, i % 2, 0:2 * P], ident_bf[:], unseen[:], start=False, stop=True)
                last.then_inc(s_ps, 1)

            def transpose_probs(c, i):
                upto(pe, p_done, BT * c + i + 1)
                if i == 0:
                    upto(pe, v_done, 2 * c + 2)
                else:
                    upto(pe, pt_done, 12 * c + PT_AT[i])
                nb = BT - i
                for m in range((nb + 3) // 4):
                    for j in range(4 * m, min(nb, 4 * m + 4)):
                        last = pe.transpose(mid[:, m, P * (j % 4):P * (j % 4) + P],
                                            prob[:, i % 2, P * j:P * j + P], ident[:])
                    last.then_inc(pt_ps, 1)

            def sum_values(c):
                upto(pe, acc_done, BT * c)
                for j in range(BT - 1):
                    last = pe.matmul(o_ps_t[:, 0:2], v[:, j, :], ones2[:], start=(j == 0), stop=(j == BT - 2))
                last.then_inc(vs_ps, 1)

            def values(c, i):
                upto(pe, pt_done, 12 * c + PT_AT[i + 1])
                if i == 0:
                    upto(pe, vs_done, c + 1)
                else:
                    upto(pe, acc_done, BT * c + i)
                nb = BT - i
                for j in range(nb):
                    last = pe.matmul(o_ps_t[:, 0:D], probT[:, i % 2, P * j:P * j + P], v[:, i + j, :],
                                     start=(j == 0), stop=(j == nb - 1 and i < BT - 1))
                if i == BT - 1:
                    last = pe.matmul(o_ps_t[:, 0:D], vs_pad[:], ident[:], start=False, stop=True)
                last.then_inc(o_ps, 1)

            def count_members(r):
                upto(pe, route, ROUTE * r + SEEN)
                pe.matmul(rt_ps_t[:, 0:E], ones_bf[:], seen[:], start=True, stop=True).then_inc(cnt_ps, 1)

            def attend(c, r, count=False):
                transpose_probs(c, 0)
                scores(c, 2)
                sum_values(c)
                if r is not None:
                    rows_T(r, 0)
                transpose_probs(c, 1)
                if r is not None:
                    rows_T(r, 1)
                scores(c, 3)
                values(c, 0)
                if r is not None:
                    logits(r)
                transpose_probs(c, 2)
                scores(c, 4)
                comb_T(c)
                values(c, 1)
                transpose_probs(c, 3)
                scores(c, 5)
                values(c, 2)
                transpose_probs(c, 4)
                scores(c, 6)
                expert_bias(c)
                if r is not None:
                    ranks(r)
                values(c, 3)
                transpose_probs(c, 5)
                scores(c, 7)
                values(c, 4)
                transpose_probs(c, 6)
                if r is not None:
                    project_qk(r, 0)
                transpose_probs(c, 7)
                if count:
                    count_members(r)
                values(c, 5)
                if r is not None:
                    project_qk(r, 1)
                values(c, 6)
                if r is not None:
                    scores(r, 0)
                values(c, 7)
                if r is not None:
                    project_v(r)
                    scores(r, 1)
            def fold_weights():
                pe.matmul(o_ps_t[:, 0:D], wqkv_s[:, 2, :], wo_s[:], start=True, stop=True)
                pe.matmul(o_ps_t[0:E + 1, D:2 * D], bv_last[:], wo_s[:], start=True, stop=True).then_inc(w_ps, 1)

            with pe.Fori(0, 6) as _:
                for _ in range(8):
                    pe.matmul(o_ps_t[:, 0:2 * P], ident_bf[:], unseen[:], start=True, stop=True)
            rows_T(0, 0)
            rows_T(0, 1)
            pe.wait_ge(const_loaded, 16 * NCONST)
            pe.wait_ge(dve_const, DVE_CONST)
            fold_weights()
            logits(0)
            project_qk(0, 0)
            project_qk(0, 1)
            pe.wait_ge(w_done, 2)
            ranks(0)
            scores(0, 0)
            scores(0, 1)
            project_v(0)
            with pe.Fori(0, BATCHES - 2) as c:
                attend(c, c + 1)
            attend(BATCHES - 2, BATCHES - 1, count=True)
            attend(BATCHES - 1, None)

            def tile_T(it, u):
                n = it * U + u
                pe.wait_ge(rows_in[u], 16 * it + 16)
                upto(pe, xg_done, n - 1)
                pe.transpose(big[:, u % 2, 0:P], xg[:, u, 0:D], ident[:]).then_inc(xg_ps, 1)

            def tile_H(it, u):
                n = it * U + u
                upto(pe, xg_done, n + 1)
                pe.wait_ge(weights_in[u], 16 * it + 16)
                upto(pe, l_done, n - 1)
                pe.matmul(big[:, u % 2, 512:512 + P], wx[:, u, 0:D], xgT[:, u % 2, :], start=True, stop=True)
                pe.matmul(big[:, u % 2, 512 + P:512 + 2 * P], wx[:, u, D:2 * D], xgT[:, u % 2, :],
                          start=True, stop=True).then_inc(h_ps, 1)

            def tile_Y(it, u):
                n = it * U + u
                upto(pe, hw_done, n + 1)
                upto(pe, y_done, n - 1)
                pe.matmul(mid[:, u % 2, 0:D], hw[:, u % 2, :], wx[:, u, 2 * D:3 * D],
                          start=True, stop=True).then_inc(y_ps, 1)

            upto(pe, p_done, BT * BATCHES)
            upto(pe, pt_done, 12 * BATCHES)
            def step(it, u):
                for stage, ahead in ((tile_H, 3), (tile_T, 5), (tile_Y, 1)):
                    if not isinstance(it, int) or 0 <= it * U + u + ahead < SLOT_TILES:
                        stage(it + (u + ahead) // U, (u + ahead) % U)

            for u in range(-AHEAD, 0):
                step(0, u)
            with pe.Fori(0, SLOT_TILES // U - 1) as it:
                for u in range(U):
                    step(it, u)
            for u in range(U):
                step(SLOT_TILES // U - 1, u)

        @block.scalar
        def _(act):
            act.wait_ge(const_loaded, 16 * NCONST)
            act.wait_ge(dve_const, DVE_CONST)

            head_start(act, v_done, vs_done, xnT_done, rs_done, tt_done, qk_done, ex_done, pay_done, p_done, pt_done, ct_done, xg_done, sl_done, y_done)

            def rows_T(r, g):
                upto(act, xnT_ps, 2 * r + g + 1)
                act.copy(xnT[:, 512 * g:512 * g + 512], rt_ps_t[:]).then_inc(xnT_done, 1)

            def row_scales(r):
                act.copy(rs_b[:], stat[:, 2, bass.ds(r * BT, BT)]).then_inc(rs_done, 1)

            def rms_rows(r):
                upto(act, rs_done, r + 1)
                upto(act, pay_done, BT * r)
                for j in range(BT):
                    act.activation(tt[:, j, :], xn[:, j, :], ACT.Copy, scale=rs_b[:, j:j + 1]).then_inc(tt_done, 1)

            def payload(r, j, free=None):
                if free is not None:
                    act.wait_ge(pay_free, free)
                if j == 0:
                    upto(act, tt_done, BT * r + BT)
                act.copy(pay[:, K * j:K * j + K, 0:D], bcast(tt[:, j, :].unsqueeze(1), [P, K, D])).then_inc(pay_done, 1)

            def top_exp(r):
                upto(act, route, ROUTE * r + DLT)
                act.activation(ex[:], dlt[:], ACT.Exp).then_inc(ex_done, 1)
                act.activation(elg[:], elg[:], ACT.Exp).then_inc(ex_done, 1)

            def comb_T(r):
                for g in range(2):
                    upto(act, ct_ps, 2 * r + g + 1)
                    act.copy(combT[:, 512 * g:512 * g + 512], big[0:E + 1, g, 512:1024])\
                       .then_inc(ct_done, 1)

            def qk(c, g, w):
                upto(act, qk_ps, 4 * c + 2 * g + w + 1)
                act.activation((qT, kT)[w][:, 512 * g:512 * g + 512], big[:, w, 512:1024], ACT.Identity,
                               bias=(bq_scaled[:, 0:1], bias_s[:, 1:2])[w], scale=(SCALE, 1.0)[w]).then_inc(qk_done, 1)

            def v_in(r, g):
                upto(act, v_ps, 2 * r + g + 1)
                act.copy(v[:, 4 * g:4 * g + 4, :], mid[:, 1 - g, :].rearrange("p (j d) -> p j d", d=D))\
                   .then_inc(v_done, 1)

            def v_sum(c):
                upto(act, vs_ps, c + 1)
                act.copy(vs_pad[:, P - 2:P], o_ps_t[:, 0:2]).then_inc(vs_done, 1)

            def exps(c, i):
                upto(act, smax, BT * c + i + 1)
                upto(act, pt_ps, 12 * c + (PT_AT[i - 1] if i >= 2 else 0))
                w = SEQ - P * i
                act.activation(prob[:, i % 2, 0:w], big[:, i % 2, 0:w], ACT.Exp, bias=neg_m[:, i:i + 1],
                               accum_out=rsum[:, i:i + 1]).then_inc(p_done, 1)

            def probs_T(c, i):
                upto(act, o_ps, BT * c + max(i - 1, 0))
                nb = BT - i
                for m in range((nb + 3) // 4):
                    n = P * min(4, nb - 4 * m)
                    upto(act, pt_ps, 12 * c + PT_AT[i] + m + 1)
                    act.copy(probT[:, i % 2, 512 * m:512 * m + n], mid[:, m, 0:n]).then_inc(pt_done, 1)

            def attend(c, r):
                probs_T(c, 0)
                exps(c, 1)
                if r is not None:
                    rows_T(r, 0)
                    rows_T(r, 1)
                v_sum(c)
                exps(c, 2)
                if r is not None:
                    row_scales(r)
                probs_T(c, 1)
                exps(c, 3)
                probs_T(c, 2)
                if r is not None:
                    rms_rows(r)
                exps(c, 4)
                probs_T(c, 3)
                if r is not None:
                    top_exp(r)
                    payload(r, 0, 2 * c + 1)
                comb_T(c)
                if r is not None:
                    payload(r, 1)
                    payload(r, 2)
                probs_T(c, 4)
                exps(c, 5)
                probs_T(c, 5)
                exps(c, 6)
                probs_T(c, 6)
                exps(c, 7)
                if r is not None:
                    qk(r, 0, 0)
                    qk(r, 0, 1)
                    payload(r, 3)
                    qk(r, 1, 0)
                probs_T(c, 7)
                if r is not None:
                    qk(r, 1, 1)
                    payload(r, 4, 2 * c + 2)
                    payload(r, 5)
                    v_in(r, 0)
                    v_in(r, 1)
                    exps(r, 0)
                    payload(r, 6)
                    payload(r, 7)
            rows_T(0, 0)
            rows_T(0, 1)
            row_scales(0)
            rms_rows(0)
            qk(0, 0, 0)
            qk(0, 0, 1)
            payload(0, 0)
            payload(0, 1)
            top_exp(0)
            payload(0, 2)
            qk(0, 1, 0)
            qk(0, 1, 1)
            v_in(0, 0)
            v_in(0, 1)
            payload(0, 3)
            exps(0, 0)
            payload(0, 4)
            payload(0, 5)
            payload(0, 6)
            payload(0, 7)
            with act.Fori(0, BATCHES - 1) as c:
                attend(c, c + 1)
            attend(BATCHES - 1, None)

            def tile_X(it, u):
                n = it * U + u
                upto(act, xg_ps, n + 1)
                upto(act, h_ps, n - 1)
                act.activation(xgT[:, u % 2, :], big[:, u % 2, 0:P], ACT.Copy, scale=bias_s[:, 2:3]).then_inc(xg_done, 1)

            def tile_S(it, u):
                n = it * U + u
                upto(act, g_done, n + 1)
                upto(act, hw_done, n - 1)
                act.activation(sl[:, u % 2, :], hg[:, u % 2, :], ACT.Silu, scale=ALPHA).then_inc(sl_done, 1)

            def tile_E(it, u):
                n = it * U + u
                upto(act, y_ps, n + 1)
                act.activation(ye[:, u, :], mid[:, u % 2, 0:D], ACT.Copy, scale=xg[:, u, WEIGHT:WEIGHT + 1])\
                   .then_inc(y_done, 1)

            def step(it, u):
                for stage, ahead in ((tile_E, 0), (tile_X, 4), (tile_S, 2)):
                    if not isinstance(it, int) or 0 <= it * U + u + ahead < SLOT_TILES:
                        stage(it + (u + ahead) // U, (u + ahead) % U)

            for u in range(-AHEAD, 0):
                step(0, u)
            act.wait_ge(plan_back, 16)
            at_reg = [act.alloc_register(f"at_reg{n}") for n in range(len(ACT_SLOTS))]
            plan_v = plan_row[:, 0:2 * SLOT_TILES].rearrange("a (t m) -> a t m", m=2 * U)
            with act.Fori(0, SLOT_TILES // U - 1) as it:
                act.reg_load(at_reg, plan_v[0:1, bass.ds(it + 1, 1), 2 * ACT_SLOTS[0] + 1:2 * ACT_SLOTS[-1] + 2:2 * ACT_SLOTS.step]
                             .rearrange("a b n -> a (b n)"))
                for u in range(U):
                    step(it, u)
                    if u - LAG in ACT_SLOTS:
                        w = u - LAG
                        act.wait_ge(returned[w], 16 * it + 16)
                        at = act.snap(at_reg[ACT_SLOTS.index(w)], min_val=0, max_val=DUMMY)
                        act.dma_start(xg[:, w, :], slots[bass.ds(at, P), :]).then_inc(rows_in[w], 16)
            for u in range(U):
                step(SLOT_TILES // U - 1, u)

            out_v = out.rearrange("(i p) d -> p i d", p=P)
            for q in range(TILES // CH):
                act.wait_ge(summed, 3 * q + 3)
                act.dma_start(out_v[:, q * CH:(q + 1) * CH, :], xs[:, q * CH:(q + 1) * CH, :]).then_inc(stored, 16)
            act.wait_ge(stored, 16 * (TILES // CH))

        @block.vector
        def _(dve):
            n_const = [0]

            def const(ins):
                n_const[0] += 1
                ins.then_inc(dve_const, 1)

            const(dve.memset(ones2[:], 1.0))
            const(dve.memset(seen[:], 0.0))
            const(dve.memset(comb[:], 0.0))
            dve.wait_ge(dve_const, n_const[0])
            const(dve.memset(comb[:, :, E:E + 1], 1.0))

            n_stat = [0]

            def stat_step(ins, wait=True):
                n_stat[0] += 1
                ins.then_inc(stats, 1)
                if wait:
                    dve.wait_ge(stats, n_stat[0])

            def moments(b0, b1):
                for b in range(b0, b1):
                    dve.wait_ge(x_loaded[b], 16)
                    for j in range(BT):
                        stat_step(dve.bn_stats(bnst[:, j, :], xs[:, b * BT + j, :]), j == BT - 1)
                    for j in range(BT):
                        stat_step(dve.bn_aggr(mv[:, b * BT + j, :], bnst[:, j, :]), j == BT - 1)

            def scales(b0, b1):
                cols = slice(b0 * BT, b1 * BT)
                var, a, a_rms = mv[:, cols, 1], nu[:, 0, cols], nu[:, 1, cols]
                stat_step(dve.tensor_copy(stat[:, 0, cols], mv[:, cols, 0]), False)
                stat_step(dve.tensor_scalar(a, var, EPS, None, ALU.add))
                stat_step(dve.reciprocal(nh[:, 0, cols], a), False)
                stat_step(dve.scalar_tensor_tensor(a_rms, a, EPS, var, ALU.mult, ALU.add))
                stat_step(dve.tensor_tensor(a_rms, a_rms, nh[:, 0, cols], ALU.mult))
                a2, bits, half, t, dst = nu[:, :, cols], nbits[:, :, cols], nh[:, :, cols], nv[:, :, cols], stat[:, 1:3, cols]
                stat_step(dve.tensor_scalar(bits, a2.bitcast(I32), -0.5, float(0x5F3759DF), ALU.mult, ALU.add), False)
                stat_step(dve.tensor_scalar(half, a2, -0.5, None, ALU.mult))
                guess = bits.bitcast(F32)
                for _ in range(3):
                    stat_step(dve.tensor_tensor(t, guess, guess, ALU.mult))
                    stat_step(dve.tensor_tensor(t, t, half, ALU.mult))
                    stat_step(dve.scalar_tensor_tensor(dst, t, 1.5, guess, ALU.add, ALU.mult))
                    guess = dst

            head_start(dve, xn_done, base_done, st_done, lg_done, top_done, route, masked, smax,
                       den_done, acc_done, b2_added, g_done, b1p_done, l_done, hw_done)

            def own(r, k):
                upto(dve, route, ROUTE * r + k)

            def normalise(r):
                dve.tensor_copy(st_b[:], stat[:, :, bass.ds(r * BT, BT)]).then_inc(st_done, 1)
                upto(dve, st_done, r + 1)
                upto(dve, tt_done, BT * r)
                for j in range(BT):
                    dve.tensor_scalar(xn[:, j, :], xs[:, bass.ds(r * BT + j, 1), :].rearrange("p a d -> p (a d)"),
                                      st_b[:, 0, j:j + 1], st_b[:, 1, j:j + 1], ALU.subtract, ALU.mult)\
                       .then_inc(xn_done, 1)

            def start_output(r):
                upto(dve, xn_done, BT * r + BT)
                rows = xs[:, bass.ds(r * BT, BT), :]
                dve.tensor_tensor(rows, rows, xn[:], ALU.add).then_inc(base_done, 1)

            def gate(r):
                upto(dve, lg_ps, r + 1)
                dve.tensor_tensor(lg[:], lg_ps_v, bcast(st_b[:, 2, :].unsqueeze(2), [P, BT, E]), ALU.mult)\
                   .then_inc(lg_done, 1)
                upto(dve, lg_done, 2 * r + 1)
                dve.tensor_tensor(lg[:], lg[:], bcast(gate_b_b[:].unsqueeze(1), [P, BT, E]), ALU.add)\
                   .then_inc(lg_done, 1)

            def top(r):
                upto(dve, lg_done, 2 * r + 2)
                dve.sem_inc(dve_go, 1)
                for j in range(BT):
                    dve.max(mx[:, j, :], lg[:, j, :]).then_inc(top_done, 1)

            def top_index(r):
                upto(dve, top_done, 2 * BT * r + BT)
                dve.sem_inc(dve_go, 1)
                for j in range(BT):
                    dve.max_index(mi[:, j, :], mx[:, j, :], lg[:, j, :]).then_inc(top_done, 1)
                dve.tensor_tensor(dlt[:], mx[:, :, 0:K], bcast(mx[:, :, 0:1], [P, BT, K]), ALU.subtract)\
                   .then_inc(route, 1)
                dve.tensor_tensor(elg[:], lg[:], bcast(mx[:, :, 0:1], [P, BT, E]), ALU.subtract)\
                   .then_inc(route, 1)
                upto(dve, top_done, 2 * BT * r + 2 * BT)
                dve.tensor_copy(idxf[:], mi[:, :, 0:K]).then_inc(route, 1)

            def one_hot(r):
                own(r, 3)
                dve.tensor_tensor(onehot[:], bcast(iota_e[:].unsqueeze(1), [P, SPREAD, E]),
                                  bcast(idxf[:].rearrange("p j k -> p (j k)").unsqueeze(2), [P, SPREAD, E]),
                                  ALU.is_equal).then_inc(route, 1)

            def members(r):
                own(r, 4)
                hot = onehot[:].rearrange("p (j k) e -> p j k e", k=K)
                dve.tensor_tensor(pairs[:], hot[:, :, 0:2, :], hot[:, :, 2:4, :], ALU.add).then_inc(route, 1)
                own(r, 5)
                dve.tensor_tensor(member[:], pairs[:, :, 0, :], pairs[:, :, 1, :], ALU.add).then_inc(route, 1)

            def members_sum(r):
                own(r, 6)
                dve.tensor_reduce(seen_add[:], member[:].rearrange("p j e -> p e j"), AX.X, ALU.add)\
                   .then_inc(route, 1)

            def slot_ranks(r):
                own(r, 7)
                upto(dve, rank_ps, r + 1)
                dve.tensor_tensor(cw[:].rearrange("p (j k) e -> p j k e", k=K),
                                  onehot[:].rearrange("p (j k) e -> p j k e", k=K),
                                  bcast(rank_ps_v.unsqueeze(2), [P, BT, K, E]), ALU.mult).then_inc(route, 1)
                dve.tensor_tensor(seen[:], seen[:], seen_add[:], ALU.add).then_inc(route, 1)
                own(r, 8)
                dve.tensor_reduce(rank[:], cw[:], AX.X, ALU.add).then_inc(route, 1)

            def weights(r):
                upto(dve, ex_done, 2 * r + 2)
                dve.tensor_reduce(esum[:], ex[:], AX.X, ALU.add).then_inc(route, 1)
                own(r, 11)
                dve.reciprocal(erec[:], esum[:]).then_inc(route, 1)
                own(r, 12)
                dve.tensor_tensor(wk[:], ex[:], bcast(erec[:].unsqueeze(2), [P, BT, K]), ALU.mult)\
                   .then_inc(route, 1)

            def combine(r):
                dve.tensor_tensor(elg[:], elg[:], bcast(erec[:].unsqueeze(2), [P, BT, E]), ALU.mult)\
                   .then_inc(route, 1)
                own(r, 22)
                dve.tensor_tensor(comb[:, :, 0:E], elg[:], member[:], ALU.mult).then_inc(route, 1)

            def address(r, g, free):
                n = slice(HALF * g, HALF * g + HALF)
                own(r, 13)
                if free is not None:
                    dve.wait_ge(pay_free, free)
                dve.tensor_scalar(pay[:, n, WEIGHT:WEIGHT + 1],
                                  wk[:].rearrange("p j k -> p (j k)")[:, n].unsqueeze(2), 1.0 / ALPHA, None, ALU.mult)\
                   .then_inc(route, 1)
                dve.tensor_copy(pay[:, n, DEST:DEST + 1].bitcast(I32), ids[:, n].unsqueeze(2))\
                   .then_inc(route, 1)
                own(r, 15 + 4 * g)
                dve.tensor_scalar(ids[:, n], ids[:, n], float(K * SEQ), None, ALU.add).then_inc(route, 1)
                dve.scalar_tensor_tensor(pos[:, n], idxf[:].rearrange("p j k -> p (j k)")[:, n], float(CAP),
                                         rank[:, n], ALU.mult, ALU.add).then_inc(route, 1)

            def add_bias(c, g):
                upto(dve, b2_ps, 2 * c + g + 1)
                if g == 0:
                    upto(dve, acc_done, BT * c + 4)
                rows = xs[:, bass.ds(c * BT + 4 * g, 4), :]
                dve.tensor_tensor(rows, rows, big[:, g, 512:1024].rearrange("p (j d) -> p j d", d=D), ALU.add)\
                   .then_inc(b2_added, 1)

            def row_max(c, i):
                w = SEQ - P * i
                upto(dve, s_ps, BT * c + i + 1)
                if i == BT - 1:
                    dve.tensor_tensor(big[:, i % 2, 0:P], big[:, i % 2, 0:P], cap_mask[:], ALU.min)\
                       .then_inc(masked, 1)
                    upto(dve, masked, c + 1)
                dve.tensor_reduce(neg_m[:, i:i + 1], big[:, i % 2, 0:w], AX.X, ALU.max, negate=True).then_inc(smax, 1)

            def add_attention(c, k):
                if k == 0:
                    upto(dve, base_done, c + 1)
                if k >= 4:
                    upto(dve, b2_added, 2 * c + 2)
                upto(dve, o_ps, BT * c + k + 1)
                if k == BT - 1:
                    dve.tensor_tensor(rsum[:, k:k + 1], rsum[:, k:k + 1], extra[:], ALU.add).then_inc(den_done, 1)
                    upto(dve, den_done, (BT + 1) * c + BT)
                dve.reciprocal(rden[:, k:k + 1], rsum[:, k:k + 1]).then_inc(den_done, 1)
                upto(dve, den_done, (BT + 1) * c + k + (2 if k == BT - 1 else 1))
                row = xs[:, bass.ds(c * BT + k, 1), :].rearrange("p a d -> p (a d)")
                dve.scalar_tensor_tensor(row, o_ps_t[:, 0:D], rden[:, k:k + 1], row, ALU.mult, ALU.add)\
                   .then_inc(acc_done, 1)

            def folded_weights():
                dve.wait_ge(w_ps, 1)
                dve.tensor_copy(wvo_s[:], o_ps_t[:, 0:D]).then_inc(w_done, 1)
                dve.tensor_tensor(b2_s[:], b2_s[:], o_ps_t[0:E + 1, D:2 * D], ALU.add).then_inc(w_done, 1)

            def attend(c, r, plan=False):
                if r is not None:
                    normalise(r)
                row_max(c, 2)
                row_max(c, 3)
                if r is not None:
                    gate(r)
                add_attention(c, 0)
                if r is not None:
                    top(r)
                row_max(c, 4)
                if r is not None:
                    top_index(r)
                add_attention(c, 1)
                if r is not None:
                    start_output(r)
                    one_hot(r)
                    members(r)
                row_max(c, 5)
                row_max(c, 6)
                add_attention(c, 2)
                if r is not None:
                    members_sum(r)
                    slot_ranks(r)
                add_attention(c, 3)
                row_max(c, 7)
                add_bias(c, 0)
                add_bias(c, 1)
                if r is not None:
                    weights(r)
                add_attention(c, 4)
                if r is not None:
                    address(r, 0, 2 * c + 1)
                if plan:
                    make_plan()
                add_attention(c, 5)
                if r is not None:
                    address(r, 1, 2 * c + 2)
                add_attention(c, 6)
                add_attention(c, 7)
                if r is not None:
                    row_max(r, 0)
                    row_max(r, 1)
                    combine(r)

            n_plan = [0]

            def plan_step(ins):
                n_plan[0] += 1
                ins.then_inc(planned, 1)
                dve.wait_ge(planned, n_plan[0])

            def make_plan():
                dve.wait_ge(cnt_ps, 1)
                plan_step(dve.tensor_copy(cnt[:], rt_ps_t[:, 0:E]))
                plan_step(dve.scalar_tensor_tensor(pad_at[:], iota_e[:], float(CAP), cnt[:], ALU.mult, ALU.add))
                plan_step(dve.tensor_scalar(nt_i[:], cnt[:], float(P - 1), None, ALU.add))
                plan_step(dve.tensor_scalar(nt_s[:], nt_i[:], 7, None, ALU.logical_shift_right))
                plan_step(dve.tensor_copy(nt[:], nt_s[:]))
                plan_step(dve.tensor_tensor_scan(ct[:], one_row[:], nt[:], 0.0, ALU.mult, ALU.add))
                plan_step(dve.tensor_tensor(ge[:], bcast(ct[:].unsqueeze(1), [P, 2, E]),
                                            bcast(tile_no[:].unsqueeze(2), [P, 2, E]), ALU.is_le))
                plan_step(dve.tensor_reduce(eidx[:], ge[:], AX.X, ALU.add))
                plan_step(dve.tensor_tensor(gt[:], ge[:], bcast(nt[:].unsqueeze(1), [P, 2, E]), ALU.mult))
                plan_step(dve.tensor_reduce(excl[:], gt[:], AX.X, ALU.add))
                plan_step(dve.tensor_tensor(loc[:], tile_no[:], excl[:], ALU.subtract))
                plan_step(dve.tensor_scalar(row_f[:], eidx[:], float(CAP), None, ALU.mult))
                plan_step(dve.scalar_tensor_tensor(loc[:], loc[:], float(P), row_f[:], ALU.mult, ALU.add))
                plan_step(dve.tensor_scalar(plan[:, :, 0], eidx[:], float(E - 1), None, ALU.min))
                plan_step(dve.tensor_scalar(plan[:, :, 1], loc[:], float(DUMMY), None, ALU.min))
                assert n_plan[0] == PLAN

            moments(0, 1)
            dve.wait_ge(pool_const, PAD_READY)
            const(dve.tensor_copy(iota_e[:], iota_i[:]))
            const(dve.tensor_copy(ids[:], id_i[:]))
            const(dve.tensor_copy(tile_no[:], tile_no_i[:]))
            scales(0, 1)
            normalise(0)
            dve.wait_ge(const_loaded, 16 * NCONST)
            const(dve.tensor_scalar(gate_s[:], gate_raw[:], bias_s[:, 2:3], None, ALU.mult))
            const(dve.tensor_scalar(bq_scaled[:], bias_s[:, 0:1], SCALE, None, ALU.mult))
            const(dve.tensor_copy(bv_last[:, E:E + 1], bias_s[:, 3:4]))
            assert n_const[0] == DVE_CONST
            moments(1, 2)
            moments(2, 3)
            gate(0)
            top(0)
            top_index(0)
            one_hot(0)
            members(0)
            members_sum(0)
            folded_weights()
            slot_ranks(0)
            weights(0)
            moments(3, 4)
            address(0, 0, None)
            address(0, 1, None)
            combine(0)
            row_max(0, 0)
            row_max(0, 1)
            start_output(0)
            scales(1, BATCHES)
            with dve.Fori(0, BATCHES - 2) as c:
                attend(c, c + 1)
            attend(BATCHES - 2, BATCHES - 1, plan=True)
            attend(BATCHES - 1, None)

            def tile_HW(it, u):
                n = it * U + u
                upto(dve, sl_done, n + 1)
                upto(dve, l_done, n + 1)
                upto(dve, y_ps, n - 1)
                dve.scalar_tensor_tensor(hw[:, u % 2, :], hl[:, u % 2, :], 1.0 - LIMIT, sl[:, u % 2, :],
                                         ALU.max, ALU.mult).then_inc(hw_done, 1)

            def tile_G(it, u):
                n = it * U + u
                upto(dve, h_ps, n + 1)
                dve.tensor_scalar(b1p[:, u:u + 1], wx[:, u, 3 * D + 1:3 * D + 2], 1.0, None, ALU.add)\
                   .then_inc(b1p_done, 1)
                upto(dve, sl_done, n - 1)
                dve.tensor_scalar(hg[:, u % 2, :], big[:, u % 2, 512:512 + P], wx[:, u, 3 * D:3 * D + 1], LIMIT,
                                  ALU.add, ALU.min).then_inc(g_done, 1)
                upto(dve, b1p_done, n + 1)
                upto(dve, hw_done, n - 1)
                dve.tensor_scalar(hl[:, u % 2, :], big[:, u % 2, 512 + P:512 + 2 * P], b1p[:, u:u + 1],
                                  1.0 + LIMIT, ALU.add, ALU.min).then_inc(l_done, 1)

            def step(it, u):
                for stage, ahead in ((tile_G, 2), (tile_HW, 1)):
                    if not isinstance(it, int) or 0 <= it * U + u + ahead < SLOT_TILES:
                        stage(it + (u + ahead) // U, (u + ahead) % U)

            for u in range(-AHEAD, 0):
                step(0, u)
            with dve.Fori(0, SLOT_TILES // U - 1) as it:
                for u in range(U):
                    step(it, u)
            for u in range(U):
                step(SLOT_TILES // U - 1, u)

            for q in range(TILES // CH):
                dve.wait_ge(sum_in[q % LB], 16 * (q // LB + 1))
                y = yl[:, q % LB]
                dve.tensor_tensor(ya[:, q % 2], y[:, :, 0:2, :], y[:, :, 2:4, :], ALU.add).then_inc(summed, 1)
                dve.wait_ge(summed, 3 * q + 1)
                dve.tensor_tensor(yb[:, q % 2], ya[:, q % 2, :, 0, :], ya[:, q % 2, :, 1, :], ALU.add).then_inc(summed, 1)
                dve.wait_ge(summed, 3 * q + 2)
                rows = xs[:, q * CH:(q + 1) * CH, :]
                dve.tensor_tensor(rows, rows, yb[:, q % 2], ALU.add).then_inc(summed, 1)
                dve.wait_ge(summed, 3 * q + 3)


PAD_READY = 20
DVE_CONST = 10


def kernel(**inputs):
    import numpy as np
    import concourse.bacc as bacc
    from concourse.bass_utils import run_bass_kernel_spmd

    a = {n.replace("L0_attn_", "").replace("L0_ffn_", "f_"): np.asarray(v) for n, v in inputs.items()}
    w1 = a["f_w1"].reshape(E, D, 2, D)
    b1 = a["f_b1"].reshape(E, D, 2)
    experts = np.concatenate([w1[:, :, 0].transpose(0, 2, 1), w1[:, :, 1].transpose(0, 2, 1),
                              a["f_w2"].transpose(0, 2, 1), b1], axis=2)
    arrays = {
        "x": a["x"].reshape(TOKENS, D),
        "wqkv": np.stack([a["wq"], a["wk"], a["wv"].T], axis=1),
        "bq": a["bq"].reshape(D, 1), "bk": a["bk"].reshape(D, 1), "bv": a["bv"].reshape(D, 1), "wo": a["wo"],
        "bo": a["bo"].reshape(1, D), "norm_scale": a["f_norm_scale"].reshape(D, 1),
        "gate_wT": a["f_gate_w"].T, "gate_b": a["f_gate_b"], "experts": experts, "b2": a["f_b2"],
    }
    arrays = {n: np.ascontiguousarray(v) for n, v in arrays.items()}
    nc = bacc.Bacc("TRN2", target_bir_lowering=False, num_devices=1)
    args = [nc.dram_tensor(n, v.shape, mybir.dt.from_np(v.dtype), kind="ExternalInput").ap() for n, v in arrays.items()]
    out = nc.dram_tensor("out", (TOKENS, D), F32, kind="ExternalOutput").ap()
    layer(nc, *args, out)
    r = run_bass_kernel_spmd(nc, [arrays], core_ids=[0])
    return r.results[0]["out"].reshape(BATCHES, SEQ, D)
```
